# Optimizing a Trainium2 kernel written in Bass

```python
import numpy as np
import jax
import jax.numpy as jnp

def _softmax(x, axis=-1):
    return jax.nn.softmax(x, axis=axis)

def _gelu(x):
    return jax.nn.gelu(x, approximate=True)

def _silu(x):
    return jax.nn.silu(x)

def _sigmoid(x):
    return jax.nn.sigmoid(x)

def _layernorm(x, axis=-1, eps=1e-05):
    m = jnp.mean(x, axis=axis, keepdims=True)
    v = jnp.var(x, axis=axis, keepdims=True)
    return (x - m) / jnp.sqrt(v + eps)

def _scatter_add(tgt, idx, src, axis=0):
    return tgt.at[idx].add(src)

def _segment_sum(src, seg, n):
    return jax.ops.segment_sum(src, seg, n)
kernel_name = 'mk_xattn_ffn_d2_seqx_r4_5a370c'

def setup_inputs(seed: int=0):
    np.random.seed(seed)
    _w = jnp.asarray

    def _rec_inputs():
        import jax
        import jax.numpy as jnp
        _rk = jax.random.key(seed)
        x = -0.0003929 + 0.9999 * jax.random.normal(jax.random.fold_in(_rk, 1), (32, 128, 256), jnp.float32)
        _lenS = 128 - jax.random.randint(jax.random.fold_in(_rk, 7), (32,), 0, max(1, 128 // 4) + 1, jnp.int32)
        _lenS2 = 128 - jax.random.randint(jax.random.fold_in(_rk, 8), (32,), 0, max(1, 128 // 4) + 1, jnp.int32)
        _ctx_1024P = jax.random.normal(jax.random.fold_in(_rk, 11), (32, 16, 256), jnp.float32)
        _ctx_1024c = jax.random.dirichlet(jax.random.fold_in(_rk, 511), 0.3 * jnp.ones((16,), jnp.float32), (32, 128))
        _ctx_1024t = jnp.einsum('bsk,bkd->bsd', _ctx_1024c, _ctx_1024P)
        _ctx_1024t = _ctx_1024t * jax.lax.rsqrt(jnp.mean(jnp.square(_ctx_1024t)) + 1e-12) * 0.953939
        ctx_1024 = 2.81802e-05 + 1.00001 * (_ctx_1024t + 0.3 * jax.random.normal(jax.random.fold_in(_rk, 611), (32, 128, 256), jnp.float32))
        _validS = jnp.arange(128)[None, :] < _lenS[:, None]
        _validS2 = jnp.arange(128)[None, :] < _lenS2[:, None]
        _causal = jnp.tril(jnp.ones((128, 128), dtype=bool))
        mask_BxS_bk1 = jnp.broadcast_to(_validS[:, :], (32, 128))
        return (x, ctx_1024, mask_BxS_bk1)
    x, ctx_1024, mask_BxS_bk1 = _rec_inputs()

    def _L0_xattn_setup():
        import jax, jax.numpy as jnp
        import numpy as np
        B, L, D = (4, 1024, 256)
        key = jax.random.key(seed)
        k1, k2 = jax.random.split(key)
        Q = jax.random.normal(k1, (B, L, D), dtype=jnp.float32)
        K = jax.random.normal(k2, (B, L, D), dtype=jnp.float32)
        return {'Q': Q, 'K': K}
    _L0_xattn_all = _L0_xattn_setup()
    _L0_xattn_in = {k: v for k, v in _L0_xattn_all.items() if k in ()}
    del _L0_xattn_all

    def _L0_ffn_setup():
        import jax, jax.numpy as jnp
        import numpy as np
        TOP_K = 2
        key = jax.random.key(seed)
        k1, k2, k3, k4 = jax.random.split(key, 4)
        B, T, D, H, E = (2, 512, 256, 512, 8)
        x = jax.random.normal(k1, (B, T, D), dtype=jnp.float32)
        w12 = jax.random.normal(k2, (E, 2 * H, D), dtype=jnp.float32) * D ** (-0.5)
        w3 = jax.random.normal(k3, (E, D, H), dtype=jnp.float32) * H ** (-0.5)
        gate_w = jax.random.normal(k4, (E, D), dtype=jnp.float32) * D ** (-0.5)
        return {'x': x, 'w12': w12, 'w3': w3, 'gate_w': gate_w}
    _L0_ffn_all = _L0_ffn_setup()
    _L0_ffn_in = {k: v for k, v in _L0_ffn_all.items() if k in ('w12', 'w3', 'gate_w')}
    del _L0_ffn_all

    def _L1_xattn_setup():
        import jax, jax.numpy as jnp
        import numpy as np
        B, S, D = (16, 512, 256)
        NEG_BIG = 1000000000.0
        key0 = jax.random.key(seed)
        kq, kk, kv, km = jax.random.split(key0, 4)
        query = jax.random.normal(kq, (B, S, D), dtype=jnp.float32)
        key = jax.random.normal(kk, (B, S, D), dtype=jnp.float32)
        value = jax.random.normal(kv, (B, S, D), dtype=jnp.float32)
        mask = jax.random.randint(km, (B, S), 0, 2).astype(jnp.bool_)
        return {'query': query, 'key': key, 'value': value, 'mask': mask}
    _L1_xattn_all = _L1_xattn_setup()
    _L1_xattn_in = {k: v for k, v in _L1_xattn_all.items() if k in ()}
    del _L1_xattn_all

    def _L1_ffn_setup():
        import jax, jax.numpy as jnp
        import numpy as np
        EPS = 1e-05

        def rmsnorm(x):
            var = jnp.mean(jnp.square(x), axis=-1, keepdims=True)
            return x * jax.lax.rsqrt(var + 1e-06)

        def activation_quant(x):
            scale = 127.0 / jnp.clip(jnp.max(jnp.abs(x), axis=-1, keepdims=True), EPS, None)
            return jnp.clip(jnp.round(x * scale), -128, 127) / scale

        def weight_quant(w):
            scale = 1.0 / jnp.clip(jnp.mean(jnp.abs(w)), EPS, None)
            return jnp.clip(jnp.round(w * scale), -1, 1) / scale

        def bitlinear(x, w, b):
            xn = rmsnorm(x)
            xq = xn + jax.lax.stop_gradient(activation_quant(xn) - xn)
            wq = w + jax.lax.stop_gradient(weight_quant(w) - w)
            return jnp.einsum('bsi,oi->bso', xq, wq) + b
        key = jax.random.key(seed)
        k1, k2, k3 = jax.random.split(key, 3)
        B, S, D, H = (4, 512, 256, 1024)
        x = jax.random.normal(k1, (B, S, D), dtype=jnp.float32)
        w1 = jax.random.normal(k2, (H, D), dtype=jnp.float32) * D ** (-0.5)
        b1 = jnp.zeros((H,), dtype=jnp.float32)
        w2 = jax.random.normal(k3, (D, H), dtype=jnp.float32) * H ** (-0.5)
        b2 = jnp.zeros((D,), dtype=jnp.float32)
        return {'x': x, 'w1': w1, 'b1': b1, 'w2': w2, 'b2': b2}
    _L1_ffn_all = _L1_ffn_setup()
    _L1_ffn_in = {k: v for k, v in _L1_ffn_all.items() if k in ('w1', 'b1', 'w2', 'b2')}
    del _L1_ffn_all
    return {'x': x, 'ctx_1024': ctx_1024, 'mask_BxS_bk1': mask_BxS_bk1, 'L0_ffn_w12': _L0_ffn_in['w12'], 'L0_ffn_w3': _L0_ffn_in['w3'], 'L0_ffn_gate_w': _L0_ffn_in['gate_w'], 'L1_ffn_w1': _L1_ffn_in['w1'], 'L1_ffn_b1': _L1_ffn_in['b1'], 'L1_ffn_w2': _L1_ffn_in['w2'], 'L1_ffn_b2': _L1_ffn_in['b2']}

def reference(x, ctx_1024, mask_BxS_bk1, L0_ffn_w12, L0_ffn_w3, L0_ffn_gate_w, L1_ffn_w1, L1_ffn_b1, L1_ffn_w2, L1_ffn_b2):
    import jax
    import jax.numpy as jnp

    def _L0_xattn_ref(Q, K):
        import jax, jax.numpy as jnp
        import numpy as np
        B, L, D = (4, 1024, 256)
        scores = jnp.einsum('btd,bsd->bts', K, K)
        Lq = Q.shape[1]
        mask = jnp.tril(jnp.ones((Lq, Lq), dtype=scores.dtype))
        scores = scores * mask[None, :, :]
        Q_proj = jnp.einsum('bts,bsd->btd', scores, Q)
        return Q + Q_proj

    def _L0_ffn_ref(x, w12, w3, gate_w):
        import jax, jax.numpy as jnp
        import numpy as np
        TOP_K = 2
        E = gate_w.shape[0]
        H = w3.shape[-1]
        scores = jnp.einsum('btd,ed->bte', x, gate_w)
        topk_scores, topk_idx = jax.lax.top_k(scores, TOP_K)
        topk_probs = jax.nn.softmax(topk_scores, axis=-1)
        total_probs = jnp.sum(jax.nn.one_hot(topk_idx, E, dtype=topk_probs.dtype) * topk_probs[..., None], axis=-2)
        h12 = jnp.einsum('btd,ehd->bteh', x, w12)
        h1, h2 = (h12[..., :H], h12[..., H:])
        hidden = jax.nn.silu(h1) * h2
        expert_out = jnp.einsum('bteh,edh->bted', hidden, w3)
        y = jnp.sum(total_probs[..., None] * expert_out, axis=-2)
        return y

    def _L1_xattn_ref(query, key, value, mask):
        import jax, jax.numpy as jnp
        import numpy as np
        B, S, D = (16, 512, 256)
        NEG_BIG = 1000000000.0
        d = query.shape[-1]
        scale = 1.0 / jnp.sqrt(jnp.asarray(d, dtype=query.dtype))
        e = jnp.einsum('bid,bjd->bij', query, key) * scale
        m = mask.astype(query.dtype)[:, :, None]
        e = e - (1.0 - m) * NEG_BIG
        a = jax.nn.softmax(e, axis=-1)
        return jnp.einsum('bij,bjd->bid', a, value)

    def _L1_ffn_ref(x, w1, b1, w2, b2):
        import jax, jax.numpy as jnp
        import numpy as np
        EPS = 1e-05

        def rmsnorm(x):
            var = jnp.mean(jnp.square(x), axis=-1, keepdims=True)
            return x * jax.lax.rsqrt(var + 1e-06)

        def activation_quant(x):
            scale = 127.0 / jnp.clip(jnp.max(jnp.abs(x), axis=-1, keepdims=True), EPS, None)
            return jnp.clip(jnp.round(x * scale), -128, 127) / scale

        def weight_quant(w):
            scale = 1.0 / jnp.clip(jnp.mean(jnp.abs(w)), EPS, None)
            return jnp.clip(jnp.round(w * scale), -1, 1) / scale

        def bitlinear(x, w, b):
            xn = rmsnorm(x)
            xq = xn + jax.lax.stop_gradient(activation_quant(xn) - xn)
            wq = w + jax.lax.stop_gradient(weight_quant(w) - w)
            return jnp.einsum('bsi,oi->bso', xq, wq) + b
        h = bitlinear(x, w1, b1)
        h = jax.nn.gelu(h, approximate=False)
        return bitlinear(h, w2, b2)
    x = x + _L0_xattn_ref(_layernorm(x, axis=-1), ctx_1024)
    x = x + _L0_ffn_ref(_layernorm(x, axis=-1), L0_ffn_w12, L0_ffn_w3, L0_ffn_gate_w)
    x = x + _L1_xattn_ref(_layernorm(x, axis=-1), ctx_1024, ctx_1024, mask_BxS_bk1)
    x = x + _L1_ffn_ref(_layernorm(x, axis=-1), L1_ffn_w1, L1_ffn_b1, L1_ffn_w2, L1_ffn_b2)
    return x

_drawn_inputs = setup_inputs


def setup_inputs(seed=0):
    import zlib

    import numpy as np

    out = dict(_drawn_inputs(seed))
    spreads = {'L1_ffn_b1': (0.0, 2.0), 'L1_ffn_b2': (0.0, 2.0)}
    factors = {'L0_ffn_w12': 8.0,
     'L0_ffn_w3': 8.0,
     'L0_ffn_gate_w': 8.0,
     'L1_ffn_w1': 64.0,
     'L1_ffn_w2': 64.0}
    for name, (base, spread) in spreads.items():
        noise = np.random.default_rng([zlib.crc32(name.encode()), seed]).standard_normal(out[name].shape)
        drawn = base * np.exp(spread * noise) if base else spread * noise
        out[name] = jnp.asarray(drawn.astype(out[name].dtype))
    for name, factor in factors.items():
        out[name] = (out[name] * factor).astype(out[name].dtype)
    return out
```

```python
from contextlib import ExitStack

import concourse.bass as bass
from concourse import mybir

ALU = mybir.AluOpType
ACT = mybir.ActivationFunctionType
DT = mybir.dt
F32, F32R, F16, BF16 = DT.float32, DT.float32r, DT.float16, DT.bfloat16
I32, U32, U8 = DT.int32, DT.uint32, DT.uint8
AX_X = mybir.AxisListType.X

P = 128
T = 32
D = 256
DC = D // P
E = 8
H = 512
HC = H // P
F = 1024
FC = F // P
Q = 4
NQ = T // Q
NB = 2 * T + E - 1
NBE = NB + 1
LN_EPS = 1e-5
RMS_EPS = 1e-6
QUANT_EPS = 1e-5
NEG_BIG = 1e9
Z_SCALE = 1024.0
ROUND = 1.5 * 2.0 ** 23
RSQRT_SEED = 0x5F3759DF
HUGE = 3e38


def after(eng, sem, count):
    if not (isinstance(count, int) and count <= 0):
        eng.wait_ge(sem, count)


def apart(eng, sem, count):
    if isinstance(count, int):
        after(eng, sem, count)
    else:
        eng.wait_ge(sem, count)
        eng.nop(nofuse=True)


class Chain:

    def __init__(self, eng, sem, start):
        self.eng, self.sem, self.start, self.n = eng, sem, start, 0

    def post(self, ins):
        ins.then_inc(self.sem, 1)
        self.n += 1

    def join(self):
        self.eng.wait_ge(self.sem, self.start + self.n)

    def link(self, ins):
        self.post(ins)
        self.join()


def rsqrt_steps(dve, chain, y, v, u):
    chain.link(dve.tensor_scalar(y.bitcast(I32), v.bitcast(I32), 1, None, ALU.logical_shift_right))
    chain.link(dve.tensor_scalar(y.bitcast(I32), y.bitcast(I32), -1, RSQRT_SEED, ALU.mult, ALU.add))
    for _ in range(3):
        chain.link(dve.tensor_tensor(u, y, y, ALU.mult))
        chain.link(dve.scalar_tensor_tensor(out=u, in0=u, scalar=-0.5, in1=v, op0=ALU.mult, op1=ALU.mult))
        chain.link(dve.scalar_tensor_tensor(out=y, in0=u, scalar=1.5, in1=y, op0=ALU.add, op1=ALU.mult))


RSQRT_N = 11


def moments(dve, chain, st, mean, var, a):
    chain.post(dve.tensor_tensor(mean, st[:, :, 1], st[:, :, 4], ALU.add))
    chain.post(dve.tensor_tensor(a, st[:, :, 1], st[:, :, 4], ALU.subtract))
    chain.link(dve.tensor_tensor(var, st[:, :, 2], st[:, :, 5], ALU.add))
    chain.post(dve.tensor_scalar(mean, mean, 0.5, None, ALU.mult))
    chain.post(dve.tensor_scalar(var, var, 1.0 / D, None, ALU.mult))
    chain.link(dve.tensor_tensor(a, a, a, ALU.mult))
    chain.link(dve.scalar_tensor_tensor(out=var, in0=a, scalar=0.25, in1=var, op0=ALU.mult, op1=ALU.add))


MOMENTS_N = 7
NORM_N = MOMENTS_N + 1 + RSQRT_N


def build(nc, x, ctx_1024, mask_BxS_bk1, L0_ffn_w12, L0_ffn_w3, L0_ffn_gate_w,
          L1_ffn_w1, L1_ffn_b1, L1_ffn_w2, L1_ffn_b2, out, upto=9, dbg=None):
    z_dram = nc.dram_tensor("z_rows", (T * P, D), F32, kind="Internal").ap()
    ye_dram = nc.dram_tensor("expert_rows", (NB * P, D), F32, kind="Internal").ap()
    xd = x.rearrange("b p d -> p b d")
    cd = ctx_1024.rearrange("b p d -> p b d")
    zd = z_dram.rearrange("(b p) d -> p b d", p=P)
    yd = ye_dram.rearrange("(b p) d -> p b d", p=P)
    od = out.rearrange("b p d -> p b d")

    whole = ExitStack()
    with whole:
        def sbw(name, shape, dt):
            return whole.enter_context(nc.sbuf_tensor(name, shape, dt))

        def sem(name):
            return whole.enter_context(nc.semaphore(name))

        PS = whole.enter_context(nc.psum_tensor("banks", [P, 8, 512], F32))

        X1 = sbw("x_rows", [P, T, D], F32)
        ident = sbw("ident", [P, P], F32)
        ones = sbw("ones", [P, P], F32)
        tri = sbw("tri", [P, P], F32)
        w1q = sbw("w1q", [P, DC, F], BF16)
        w2q = sbw("w2q", [P, FC, D], BF16)
        wmean = sbw("wmean", [P, 2], F32)
        magic = sbw("magic", [P, 2], F32)
        rowmask = sbw("rowmask", [P, T], F32)
        b1b = sbw("b1b", [P, F], F32)
        b2b = sbw("b2b", [P, D], F32)
        ye_idx = sbw("ye_idx", [P, T, 2], U32)
        prob = sbw("prob", [P, 2, T], F32)
        s_id = sem("s_id")
        s_k = sem("s_k")

        moe = ExitStack()
        whole.enter_context(moe)

        def sbm(name, shape, dt):
            return moe.enter_context(nc.sbuf_tensor(name, shape, dt))

        W12H = sbm("w12_high", [P, E, DC, 2 * H], F16)
        W12L = sbm("w12_low", [P, E, DC, 2 * H], F16)
        W3H = sbm("w3_high", [P, E, HC, D], F32R)
        W3L = sbm("w3_low", [P, E, HC, D], F32R)
        blk_inv = sbm("blk_inv", [P, NBE], F32)
        blk_exp = sbm("blk_exp", [P, NBE], I32)
        tok_idx = sbm("tok_idx", [P, NBE], U32)
        gT = sbm("gate_T", [P, DC, E], F32)
        LG = sbm("logits", [P, T, E], F32)
        wsc = sbm("w12_scale", [P, E], F32)
        winv = sbm("w12_unscale", [P, E], F32)

        scales(nc, sem, PS, X1, ident, ones, tri, magic, wmean, wsc, winv, rowmask, b1b, b2b, gT, w1q, w2q,
               mask_BxS_bk1, L0_ffn_w12, L0_ffn_gate_w, L1_ffn_w1, L1_ffn_b1, L1_ffn_w2, L1_ffn_b2)
        convert(nc, sem, PS, ident, wsc, W12H, W12L, W3H, W3L, L0_ffn_w12, L0_ffn_w3)
        attend0(nc, sem, PS, X1, ident, tri, gT, LG, xd, cd, zd)
        if upto >= 2:
            route(nc, sem, PS, ones, LG, winv, prob, ye_idx, tok_idx, blk_exp, blk_inv)
        if upto >= 3:
            experts(nc, sem, PS, ident, W12H, W12L, W3H, W3L, blk_inv, blk_exp, tok_idx, z_dram, yd)
        if dbg is not None:
            dbg_dump(nc, sem, dbg, locals())
        moe.close()
        if upto >= 4:
            attend1(nc, sem, PS, X1, ident, rowmask, prob, ye_idx, ye_dram, cd)
            bitffn(nc, sem, PS, X1, ident, magic, wmean, w1q, w2q, b1b, b2b, od)


def dbg_dump(nc, sem, dbg, env):
    s = sem("s_dbg")
    with nc.Block() as block:
        @block.sync
        def _(sp):
            n = 0
            for name, (dst, src) in dbg(env).items():
                sp.dma_start(dst, src).then_inc(s, 16)
                n += 16
            sp.wait_ge(s, n)


def scales(nc, sem, PS, X1, ident, ones, tri, magic, wmean, wsc, winv, rowmask, b1b, b2b, gT, w1q, w2q,
           mask, w12, gate_w, w1, b1, w2, b2):
    st = ExitStack()
    with st:
        def sb(name, shape, dt):
            return st.enter_context(nc.sbuf_tensor(name, shape, dt))

        wst = sb("w12_stage", [P, 2, 2 * H // P, D], F32)
        junk = sb("junk", [P, 2 * H // P, D], F32)
        w1s = X1[:, 0:8, :]
        w2s = X1[:, 8:16, :].rearrange("p a d -> p (a d)").rearrange("p (c f) -> p c f", c=2)
        gs = sb("gate_stage", [E, D], F32)
        ms = sb("mask_stage", [T, P], U8)
        mf = sb("mask_rows", [T, P], F32)
        ss = sb("sums", [P, E + 2], F32)
        tot = sb("totals", [P, E + 2], F32)
        ti = sb("exponents", [P, E], I32)
        tj = sb("exponents_inv", [P, E], I32)
        rec = sb("w_scale", [P, 2], F32)

        ld_w = [sem("scale_w12_in0"), sem("scale_w12_in1")]
        ld_1, ld_2, ld_g, ld_m, ld_b = sem("w1_in"), sem("w2_in"), sem("gate_in"), sem("mask_in"), sem("bias_in")
        made = sem("constants_made")
        summed = sem("w12_summed")
        abs_s = sem("w12_abs_summed")
        total = sem("totals_ready")
        tr_g, tr_m = sem("gate_turned"), sem("mask_turned")
        dch = sem("scales_dve")
        q_made = sem("ternary_made")
        q_turn = sem("ternary_turned")
        q_out = sem("ternary_kept")
        pch = sem("scales_pool")
        cast = sem("mask_cast")
        done = sem("scales_gate_out")

        w12v = w12.rearrange("e (c p) d -> p e c d", p=P)
        with nc.Block() as block:
            @block.sync
            def _(sp):
                sp.dma_start(gs[:, :], gate_w).then_inc(ld_g, 16)
                sp.dma_start(ms[:, :], mask).then_inc(ld_m, 16)
                sp.dma_start(w1s, w1.rearrange("(c p) d -> p c d", p=P)).then_inc(ld_1, 16)
                sp.dma_start(w2s, w2.rearrange("(c p) f -> p c f", p=P)).then_inc(ld_2, 16)
                sp.dma_start(b1b[:, :], b1.partition_broadcast(P)).then_inc(ld_b, 16)
                sp.dma_start(b2b[:, :], b2.partition_broadcast(P)).then_inc(ld_b, 16)
                with sp.Fori(0, E // 2) as i:
                    for u in range(2):
                        sp.wait_ge(summed, 2 * i)
                        sp.dma_start(wst[:, u, :, :], w12v[:, bass.ds(2 * i + u, 1), :, :]).then_inc(ld_w[u], 16)
                sp.wait_ge(ld_b, 32)

            @block.gpsimd
            def _(pool):
                pool.memset(ones[:, :], 1.0).then_inc(pch, 1)
                pool.memset(ident[:, :], 0.0).then_inc(pch, 1)
                pool.wait_ge(pch, 2)
                pool.affine_select(out=ident[:, :], in_=ident[:, :], compare_op=ALU.not_equal, fill=1.0,
                                   base=0, pattern=[[-1, P]], channel_multiplier=1).then_inc(made, 1)
                pool.affine_select(out=tri[:, :], in_=ones[:, :], compare_op=ALU.is_ge, fill=0.0,
                                   base=0, pattern=[[1, P]], channel_multiplier=-1).then_inc(made, 1)
                pool.memset(magic[:, 0:1], ROUND).then_inc(made, 1)
                pool.memset(magic[:, 1:2], -ROUND).then_inc(made, 1)

            @block.scalar
            def _(act):
                act.wait_ge(ld_1, 16)
                nc.scalar.activation(junk[:, :, :], w1s, ACT.Abs, accum_out=ss[:, E:E + 1]).then_inc(abs_s, 1)
                act.wait_ge(ld_2, 16)
                act.wait_ge(abs_s, 1)
                nc.scalar.activation(junk[:, :, :].rearrange("p c d -> p (c d)").rearrange("p (c f) -> p c f", c=2),
                                     w2s, ACT.Abs, accum_out=ss[:, E + 1:E + 2]).then_inc(abs_s, 1)
                with act.Fori(0, E // 2) as i:
                    for u in range(2):
                        act.wait_ge(abs_s, 2)
                        act.wait_ge(ld_w[u], 16 * i + 16)
                        act.wait_ge(summed, 2 * i + u)
                        nc.scalar.activation(junk[:, :, :], wst[:, u, :, :], ACT.Square,
                                             accum_out=ss[:, bass.ds(2 * i + u, 1)]).then_inc(summed, 1)
                for n in range(4):
                    act.wait_ge(q_turn, n + 1)
                    dst = w1q[:, n, :] if n < 2 else w2q[:, 4 * (n - 2):4 * (n - 1), :]
                    src = PS[:, 2 * n:2 * n + 2, :]
                    src = src.rearrange("p a b -> p (a b)")
                    if n >= 2:
                        src = src.rearrange("p (c d) -> p c d", d=D)
                    act.activation(dst, src, ACT.Copy).then_inc(q_out, 1)

            @block.tensor
            def _(pe):
                pe.wait_ge(made, 2)
                pe.wait_ge(ld_g, 16)
                for c in range(DC):
                    mm = pe.transpose(PS[:, 0, c * E:(c + 1) * E], gs[:, c * P:(c + 1) * P], ident[0:E, 0:E])
                mm.then_inc(tr_g, 1)
                pe.wait_ge(cast, 1)
                pe.transpose(PS[:, 1, 0:T], mf[:, :], ident[0:T, 0:T]).then_inc(tr_m, 1)
                pe.wait_ge(abs_s, 2)
                pe.wait_ge(summed, E)
                pe.matmul(PS[:, 2, 0:E + 2], ones[:, :], ss[:, :], start=True, stop=True).then_inc(total, 1)
                pe.wait_ge(dch, SCALES_TERNARY)
                pe.wait_ge(done, 2)
                for n in range(4):
                    for c in range(FC):
                        if n < 2:
                            src = w1s[:, c, n * P:(n + 1) * P]
                            o = PS[:, 2 * n + c // 4, (c % 4) * P:(c % 4 + 1) * P]
                        else:
                            h, d = 4 * (n - 2) + c // 2, c % 2
                            src = w2s[:, d, h * P:(h + 1) * P]
                            o = PS[:, 2 * n + c // 4, (c % 4) * P:(c % 4 + 1) * P]
                        mm = pe.transpose(o, src, ident[:, :])
                    mm.then_inc(q_turn, 1)

            @block.vector
            def _(dve):
                ch = Chain(dve, dch, 0)
                dve.wait_ge(ld_m, 16)
                dve.tensor_copy(mf[:, :], ms[:, :]).then_inc(cast, 1)
                dve.wait_ge(tr_g, 1)
                dve.tensor_scalar(gT[:, :, :], PS[:, 0, 0:DC * E].rearrange("p (c e) -> p c e", c=DC),
                                  1.0 / Z_SCALE, None, ALU.mult).then_inc(done, 1)
                dve.wait_ge(tr_m, 1)
                dve.tensor_scalar(rowmask[:, :], PS[:, 1, 0:T], -NEG_BIG, NEG_BIG, ALU.mult, ALU.add).then_inc(done, 1)
                dve.wait_ge(total, 1)
                ch.link(dve.tensor_copy(tot[:, :], PS[:, 2, 0:E + 2]))
                ch.link(dve.tensor_scalar(ti[:, :], tot[:, 0:E].bitcast(I32), 23, None, ALU.logical_shift_right))
                ch.link(dve.tensor_scalar(ti[:, :], ti[:, :], 1, None, ALU.add))
                ch.link(dve.tensor_scalar(ti[:, :], ti[:, :], 1, None, ALU.logical_shift_right))
                ch.post(dve.tensor_scalar(tj[:, :], ti[:, :], 39, None, ALU.add))
                ch.link(dve.tensor_scalar(ti[:, :], ti[:, :], -1, 205, ALU.mult, ALU.add))
                ch.post(dve.tensor_scalar(wsc[:, :].bitcast(I32), ti[:, :], 23, None, ALU.logical_shift_left))
                ch.post(dve.tensor_scalar(winv[:, :].bitcast(I32), tj[:, :], 23, None, ALU.logical_shift_left))
                ch.link(dve.tensor_scalar(wmean[:, :], tot[:, E:E + 2], 1.0 / (D * F), QUANT_EPS, ALU.mult, ALU.max))
                ch.link(dve.reciprocal(rec[:, :], wmean[:, :]))
                dve.wait_ge(abs_s, 2)
                dve.wait_ge(made, 4)
                for n, w in enumerate((w1s, w2s)):
                    ch.link(dve.tensor_scalar(w, w, rec[:, n:n + 1], None, ALU.mult))
                    ch.link(dve.tensor_scalar(w, w, ROUND, None, ALU.add))
                    ch.link(dve.tensor_scalar(w, w, ROUND, 1.0, ALU.subtract, ALU.min))
                    ch.link(dve.tensor_scalar(w, w, -1.0, None, ALU.max))
                assert ch.n == SCALES_TERNARY


SCALES_TERNARY = 18



def convert(nc, sem, PS, ident, wsc, W12H, W12L, W3H, W3L, w12, w3):
    st = ExitStack()
    with st:
        def sb(name, shape, dt):
            return st.enter_context(nc.sbuf_tensor(name, shape, dt))

        wst = sb("w12_rows", [P, 2, 2 * H // P, D], F32)
        vst = sb("w3_rows", [P, 2, DC, H], F32)
        in12 = [sem("w12_in0"), sem("w12_in1")]
        in3 = [sem("w3_in0"), sem("w3_in1")]
        turned, high, low = sem("w_turned"), sem("w_high"), sem("w_low")
        w12v = w12.rearrange("e (c p) d -> p e c d", p=P)
        w3v = w3.rearrange("e (c p) h -> p e c h", p=P)

        with nc.Block() as block:
            @block.sync
            def _(sp):
                def load(i, u):
                    after(sp, turned, 6 * i + 3 * u - 4)
                    sp.dma_start(wst[:, u, :, :], w12v[:, bass.ds(2 * i + u, 1), :, :]).then_inc(in12[u], 16)
                    after(sp, turned, 6 * i + 3 * u - 3)
                    sp.dma_start(vst[:, u, :, :], w3v[:, bass.ds(2 * i + u, 1), :, :]).then_inc(in3[u], 16)

                load(0, 0)
                load(0, 1)
                with sp.Fori(1, E // 2) as i:
                    load(i, 0)
                    load(i, 1)

            @block.tensor
            def _(pe):
                def turn(i, u, g):
                    after(pe, low, 6 * i + 3 * u + g - 2)
                    if g < 2:
                        pe.wait_ge(in12[u], 16 * i + 16)
                    else:
                        pe.wait_ge(in3[u], 16 * i + 16)
                    for c in range(8):
                        if g < 2:
                            src = wst[:, u, c, g * P:(g + 1) * P]
                        else:
                            src = vst[:, u, c % 2, (c // 2) * P:(c // 2 + 1) * P]
                        mm = pe.transpose(PS[:, 2 * g + c // 4, (c % 4) * P:(c % 4 + 1) * P], src, ident[:, :])
                    mm.then_inc(turned, 1)

                for u in range(2):
                    for g in range(3):
                        turn(0, u, g)
                with pe.Fori(1, E // 2) as i:
                    for u in range(2):
                        for g in range(3):
                            turn(i, u, g)

            def places(i, u, g, w12x, w3x):
                e = bass.ds(2 * i + u, 1)
                if g < 2:
                    return w12x[:, e, g, :].rearrange("p a h -> p (a h)")
                return w3x[:, e, :, :].rearrange("p a c d -> p (a c d)")

            @block.scalar
            def _(act):
                with act.Fori(0, E // 2) as i:
                    for u in range(2):
                        for g in range(3):
                            apart(act, turned, 6 * i + (3 * u + g + 1))
                            src = PS[:, 2 * g:2 * g + 2, :].rearrange("p a b -> p (a b)")
                            dst = places(i, u, g, W12H, W3H)
                            if g < 2:
                                nc.scalar.activation(dst, src, ACT.Copy, scale=wsc[:, bass.ds(2 * i + u, 1)])\
                                    .then_inc(high, 1)
                            else:
                                nc.scalar.activation(dst, src, ACT.Copy).then_inc(high, 1)

            @block.vector
            def _(dve):
                with dve.Fori(0, E // 2) as i:
                    for u in range(2):
                        for g in range(3):
                            dve.wait_ge(high, 6 * i + (3 * u + g + 1))
                            src = PS[:, 2 * g:2 * g + 2, :].rearrange("p a b -> p (a b)")
                            if g < 2:
                                nc.vector.scalar_tensor_tensor(
                                    out=places(i, u, g, W12L, W3L), in0=src, scalar=wsc[:, bass.ds(2 * i + u, 1)],
                                    in1=places(i, u, g, W12H, W3H), op0=ALU.mult, op1=ALU.subtract).then_inc(low, 1)
                            else:
                                nc.vector.tensor_tensor(
                                    places(i, u, g, W12L, W3L), src,
                                    places(i, u, g, W12H, W3H).bitcast(F32), ALU.subtract).then_inc(low, 1)


def attend0(nc, sem, PS, X1, ident, tri, gT, LG, xd, cd, zd):
    st = ExitStack()
    with st:
        def sb(name, shape, dt):
            return st.enter_context(nc.sbuf_tensor(name, shape, dt))

        xs = sb("x_in", [P, Q, D], F32)
        cs = sb("c_in", [P, Q, D], F32)
        cT = sb("c_T", [P, 2, DC * P], F32)
        y = sb("y", [P, Q, D], F32)
        xy = sb("x_plus_y", [P, Q, D], F32)
        sm = sb("scores_T", [P, Q, P], F32)
        z = sb("z", [P, Q, D], F32)
        zT = sb("z_T", [P, 2, DC * P], F32)
        stt = sb("moments_in", [P, 2 * Q, 6], F32)
        mean = sb("means", [P, 2 * Q], F32)
        var = sb("vars", [P, 2 * Q], F32)
        rst = sb("rstds", [P, 2 * Q], F32)
        tmp = sb("tmp8", [P, 2 * Q], F32)
        nsc = sb("norm_scales", [P, 2 * Q], F32)
        nbi = sb("norm_biases", [P, 2 * Q], F32)
        unit = sb("units", [P, 2 * Q], F32)

        x_in = [sem(f"x_in{k}") for k in range(Q)]
        c_in = [sem(f"c_in{k}") for k in range(Q)]
        z_out = [sem(f"z_out{k}") for k in range(Q)]
        x_stat, ct_made, ct_kept = sem("x_stat"), sem("ct_made"), sem("ct_kept")
        y_made, xy_made = sem("y_made"), sem("xy_made")
        sc_made, sm_made, qp_made, x1_made, x1_stat = (sem(n) for n in (
            "scores_made", "scores_masked", "qproj_made", "x1_made", "x1_stat"))
        z_made, zt_made, zt_kept, lg_made, lg_kept = (sem(n) for n in (
            "z_made", "zt_made", "zt_kept", "logits_made", "logits_kept"))
        norms_made, unit_made = sem("norms_made"), sem("units_made")

        with nc.Block() as block:
            @block.sync
            def _(sp):
                def load(i, k):
                    after(sp, xy_made, Q * i + (k - 3))
                    after(sp, x_stat, Q * i + (k - 3))
                    sp.dma_start(xs[:, k, :], xd[:, bass.ds(Q * i + k, 1), :]).then_inc(x_in[k], 16)
                    after(sp, ct_made, Q * i + (k - 3))
                    sp.dma_start(cs[:, k, :], cd[:, bass.ds(Q * i + k, 1), :]).then_inc(c_in[k], 16)

                def store(i, k):
                    sp.wait_ge(z_made, Q * i + (k + 1))
                    sp.dma_start(zd[:, bass.ds(Q * i + k, 1), :], z[:, k, :]).then_inc(z_out[k], 16)

                for k in range(Q):
                    load(0, k)
                with sp.Fori(1, NQ) as i:
                    for k in range(Q):
                        load(i, k)
                    for k in range(Q):
                        store(i - 1, k)
                for k in range(Q):
                    store(NQ - 1, k)
                for k in range(Q):
                    sp.wait_ge(z_out[k], 16 * NQ)

            @block.gpsimd
            def _(pool):
                def add_y(i, k):
                    after(pool, x1_made, Q * i + (k - 3))
                    pool.wait_ge(x_in[k], 16 * i + 16)
                    pool.wait_ge(y_made, Q * i + (k + 1))
                    pool.tensor_tensor(xy[:, k, :], xs[:, k, :], y[:, k, :], ALU.add).then_inc(xy_made, 1)

                for k in range(Q):
                    add_y(0, k)
                with pool.Fori(1, NQ) as i:
                    for k in range(Q):
                        add_y(i, k)

            @block.scalar
            def _(act):
                def make_y(i, k):
                    after(act, qp_made, Q * i + (k - 3))
                    act.wait_ge(norms_made, (NORM_N + 2) * i + (NORM_N + 2))
                    act.wait_ge(x_in[k], 16 * i + 16)
                    nc.scalar.activation(y[:, k, :], xs[:, k, :], ACT.Identity, scale=nsc[:, Q + k:Q + k + 1],
                                         bias=nbi[:, Q + k:Q + k + 1]).then_inc(y_made, 1)

                def keep_ct(i, k):
                    after(act, sc_made, Q * i + (k - 1))
                    act.wait_ge(ct_made, Q * i + (k + 1))
                    nc.scalar.activation(cT[:, k % 2, :], PS[:, k % 2, 0:D], ACT.Copy).then_inc(ct_kept, 1)

                def make_z(i, k):
                    act.wait_ge(norms_made, 1)
                    act.wait_ge(norms_made, (NORM_N + 2) * i + 2 * (NORM_N + 2))
                    after(act, z_out[k], 16 * i)
                    after(act, zt_made, Q * i + (k - 3))
                    nc.scalar.activation(z[:, k, :], X1[:, bass.ds(Q * i + k, 1), :].rearrange("p a d -> p (a d)"),
                                         ACT.Identity, scale=nsc[:, k:k + 1], bias=nbi[:, k:k + 1]).then_inc(z_made, 1)

                def keep_zt(i, k):
                    after(act, lg_made, Q * i + (k - 1))
                    act.wait_ge(zt_made, Q * i + (k + 1))
                    nc.scalar.activation(zT[:, k % 2, :], PS[:, 6, 0:D], ACT.Copy).then_inc(zt_kept, 1)

                def group(i):
                    for k in range(Q):
                        make_y(i, k)
                    for k in range(Q):
                        keep_ct(i, k)
                        keep_zt(i - 1, k)
                    for k in range(Q):
                        make_z(i, k)

                for k in range(Q):
                    make_y(0, k)
                for k in range(Q):
                    keep_ct(0, k)
                for k in range(Q):
                    make_z(0, k)
                group(1)
                with act.Fori(2, NQ) as i:
                    group(i)
                for k in range(Q):
                    keep_zt(NQ - 1, k)

            @block.tensor
            def _(pe):
                def turn_c(i, k):
                    after(pe, ct_kept, Q * i + (k - 1))
                    pe.wait_ge(c_in[k], 16 * i + 16)
                    for c in range(DC):
                        mm = pe.transpose(PS[:, k % 2, c * P:(c + 1) * P], cs[:, k, c * P:(c + 1) * P], ident[:, :])
                    mm.then_inc(ct_made, 1)

                def scores(i, k):
                    after(pe, sm_made, Q * i + (k - 1))
                    pe.wait_ge(ct_kept, Q * i + (k + 1))
                    for c in range(DC):
                        chunk = cT[:, k % 2, c * P:(c + 1) * P]
                        mm = pe.matmul(PS[:, 2 + k % 2, 0:P], chunk, chunk, start=(c == 0), stop=(c == DC - 1))
                    mm.then_inc(sc_made, 1)

                def product(i, k):
                    after(pe, x1_made, Q * i + (k - 1))
                    pe.wait_ge(sm_made, Q * i + (k + 1))
                    pe.wait_ge(y_made, Q * i + (k + 1))
                    pe.matmul(PS[:, 4 + k % 2, 0:D], sm[:, k, :], y[:, k, :], start=True, stop=True)\
                        .then_inc(qp_made, 1)

                def turn_z(i, k):
                    after(pe, zt_kept, Q * i + k)
                    pe.wait_ge(z_made, Q * i + (k + 1))
                    for c in range(DC):
                        mm = pe.transpose(PS[:, 6, c * P:(c + 1) * P], z[:, k, c * P:(c + 1) * P], ident[:, :])
                    mm.then_inc(zt_made, 1)

                def logits(i, k):
                    if k == 0:
                        after(pe, lg_kept, i)
                    pe.wait_ge(zt_kept, Q * i + (k + 1))
                    for c in range(DC):
                        mm = pe.matmul(PS[:, 7, k * E:(k + 1) * E], zT[:, k % 2, c * P:(c + 1) * P], gT[:, c, :],
                                       start=(c == 0), stop=(c == DC - 1))
                    mm.then_inc(lg_made, 1)

                def turns(i, before):
                    for k in range(Q):
                        turn_c(i, k)
                        if before:
                            turn_z(i - 1, k)
                        if k >= 1:
                            scores(i, k - 1)
                            if before:
                                logits(i - 1, k - 1)
                    scores(i, Q - 1)
                    if before:
                        logits(i - 1, Q - 1)
                    for k in range(Q):
                        product(i, k)

                turns(0, False)
                with pe.Fori(1, NQ) as i:
                    turns(i, True)
                for k in range(Q):
                    turn_z(NQ - 1, k)
                    logits(NQ - 1, k)

            @block.vector
            def _(dve):
                def x_moments(i, k):
                    dve.wait_ge(x_in[k], 16 * i + 16)
                    nc.vector.bn_stats(stt[:, Q + k, :], xs[:, k, :]).then_inc(x_stat, 1)

                def mask_scores(i, k):
                    after(dve, qp_made, Q * i + (k - 3))
                    dve.wait_ge(sc_made, Q * i + (k + 1))
                    nc.vector.tensor_tensor(sm[:, k, :], PS[:, 2 + k % 2, 0:P], tri[:, :], ALU.mult)\
                        .then_inc(sm_made, 1)

                def add_product(i, k):
                    dve.wait_ge(qp_made, Q * i + (k + 1))
                    dve.wait_ge(xy_made, Q * i + (k + 1))
                    nc.vector.tensor_tensor(X1[:, bass.ds(Q * i + k, 1), :].rearrange("p a d -> p (a d)"),
                                            PS[:, 4 + k % 2, 0:D], xy[:, k, :], ALU.add).then_inc(x1_made, 1)

                def x1_moments(i, k):
                    apart(dve, x1_made, Q * i + (k + 1))
                    nc.vector.bn_stats(stt[:, k, :], X1[:, bass.ds(Q * i + k, 1), :].rearrange("p a d -> p (a d)"))\
                        .then_inc(x1_stat, 1)

                def norms(start, lo, hi):
                    ch = Chain(dve, norms_made, start)
                    m, v, r, u = (a[:, lo:hi] for a in (mean, var, rst, tmp))
                    moments(nc.vector, ch, stt[:, lo:hi, :], m, v, u)
                    ch.link(nc.vector.tensor_scalar(v, v, LN_EPS, None, ALU.add))
                    rsqrt_steps(nc.vector, ch, r, v, u)
                    ch.link(nc.vector.tensor_tensor(nsc[:, lo:hi], r, unit[:, lo:hi], ALU.mult))
                    ch.link(nc.vector.scalar_tensor_tensor(out=nbi[:, lo:hi], in0=m, scalar=-1.0, in1=nsc[:, lo:hi],
                                                           op0=ALU.mult, op1=ALU.mult))
                    assert ch.n == NORM_N + 2

                def keep_logits(i):
                    dve.wait_ge(lg_made, Q * i + Q)
                    nc.vector.tensor_copy(LG[:, i * Q:(i + 1) * Q, :] if isinstance(i, int) else
                                          LG[:, bass.ds(i * Q, Q), :],
                                          PS[:, 7, 0:Q * E].rearrange("p (t e) -> p t e", t=Q)).then_inc(lg_kept, 1)

                def group(i, first=False, final=False):
                    for k in range(Q):
                        mask_scores(i, k)
                    if not final:
                        for k in range(Q):
                            x_moments(i + 1, k)
                    for k in range(Q):
                        add_product(i, k)
                        if k >= 1:
                            x1_moments(i, k - 1)
                    x1_moments(i, Q - 1)
                    dve.wait_ge(x1_stat, Q * i + Q)
                    if not final:
                        dve.wait_ge(x_stat, Q * i + 2 * Q)
                    dve.wait_ge(y_made, Q * i + Q)
                    after(dve, z_made, Q * i)
                    norms((NORM_N + 2) * (i + 1), 0, Q if final else 2 * Q)
                    if not first:
                        keep_logits(i - 1)

                nc.vector.memset(unit[:, 0:Q], Z_SCALE).then_inc(unit_made, 1)
                nc.vector.memset(unit[:, Q:2 * Q], 1.0).then_inc(unit_made, 1)
                for k in range(Q):
                    x_moments(0, k)
                dve.wait_ge(unit_made, 2)
                dve.wait_ge(x_stat, Q)
                norms(0, Q, 2 * Q)
                group(0, first=True)
                with dve.Fori(1, NQ - 1) as i:
                    group(i)
                group(NQ - 1, final=True)
                keep_logits(NQ - 1)
                dve.wait_ge(lg_kept, NQ)


def route(nc, sem, PS, ones, LG, winv, prob, ye_idx, tok_idx, blk_exp, blk_inv):
    st = ExitStack()
    with st:
        def sb(name, shape, dt=F32):
            return st.enter_context(nc.sbuf_tensor(name, shape, dt))

        rev = sb("rev_expert", [P, T, E])
        col = sb("column", [P, P])
        tok = sb("token_id", [P, T, 2])
        lower = sb("lower", [P, P])
        edge = sb("edges", [P, E, T])
        one8 = sb("ones8", [P, E * T])
        eid = sb("expert_id", [P, NBE, E])
        jid = sb("block_id", [P, NBE, E])
        first = sb("first", [P, T, E])
        second = sb("second", [P, T, E])
        both = sb("both", [P, T, E])
        a1 = sb("work1", [P, T, E])
        a2 = sb("work2", [P, T, E])
        m1, m2, c1, dl, e2, r2 = (sb(n, [P, T]) for n in ("max1", "max2", "code", "gap", "exp_gap", "rsum"))
        tile_n = sb("tile_counts", [P, E, T])
        incl = sb("inclusive", [P, E, T])
        excl = sb("exclusive", [P, E, T])
        tot, nblk, bend, base = (sb(n, [P, E]) for n in ("totals8", "blocks8", "block_end", "base8"))
        pos = sb("places", [P, T, 2])
        posi = sb("places_int", [P, 2 * T], I32)
        part = sb("places_part", [P, 2 * T], I32)
        low = sb("place_low", [P, 2 * T])
        high = sb("place_high", [P, 2 * T])
        b1_, b2_ = sb("block_work1", [P, NBE, E]), sb("block_work2", [P, NBE, E])
        be = sb("block_expert_f", [P, NBE])
        lo_hot = sb("low_hot", [P, Q, P], F32R)
        hi_hot = sb("high_hot", [P, Q, NBE], F32R)

        made = sem("route_constants")
        dch = sem("route_dve")
        gap, exped = sem("gap_ready"), sem("gap_exped")
        counted = sem("counted")
        hot, placed = sem("hot_made"), sem("placed")
        listed = sem("listed")

        with nc.Block() as block:
            @block.gpsimd
            def _(pool):
                def iota(ap, pattern, base, mult):
                    pool.iota(ap, pattern, base=base, channel_multiplier=mult,
                              allow_small_or_imprecise_dtypes=True).then_inc(made, 1)

                iota(rev[:, :, :], [[0, T], [-1, E]], E, 0)
                iota(col[:, :], [[1, P]], 0, 0)
                iota(tok[:, :, :], [[P, T], [0, 2]], 0, 1)
                iota(edge[:, :, :], [[0, E], [P, T]], 0, 0)
                iota(eid[:, :, :], [[0, NBE], [1, E]], 0, 0)
                iota(jid[:, :, :], [[1, NBE], [0, E]], 0, 0)
                pool.memset(one8[:, :], 1.0).then_inc(made, 1)
                pool.affine_select(out=lower[:, :], in_=ones[:, :], compare_op=ALU.is_gt, fill=0.0,
                                   base=0, pattern=[[1, P]], channel_multiplier=-1).then_inc(made, 1)

            @block.scalar
            def _(act):
                act.wait_ge(gap, 1)
                act.activation(e2[:, :], dl[:, :], ACT.Exp).then_inc(exped, 1)

            @block.tensor
            def _(pe):
                pe.wait_ge(made, 8)
                pe.wait_ge(dch, ROUTE_BOTH)
                flat = both[:, :, :].rearrange("p t e -> p (t e)")
                pe.matmul(PS[:, 0, 0:T * E], lower[:, :], flat, start=True, stop=True).then_inc(counted, 1)
                pe.matmul(PS[:, 1, 0:T * E], ones[:, :], flat, start=True, stop=True).then_inc(counted, 1)

                def place(n, u, start=False, stop=False):
                    pe.wait_ge(hot, 2 * n + 2)
                    pe.matmul(PS[:, 2, 0:NBE], lo_hot[:, u, :], hi_hot[:, u, :], start=start, stop=stop,
                              skip_group_check=True).then_inc(placed, 1)

                for u in range(Q):
                    place(u, u, start=(u == 0))
                with pe.Fori(1, 2 * T // Q - 1) as i:
                    for u in range(Q):
                        place(Q * i + u, u)
                for u in range(Q):
                    place(2 * T - Q + u, u, stop=(u == Q - 1))

            @block.vector
            def _(dve):
                ch = Chain(dve, dch, 0)
                v = nc.vector

                def over_e(a):
                    return a.unsqueeze(2).broadcast_to([P, T, E])

                def over_t(a):
                    return a.unsqueeze(2).broadcast_to([P, E, T])

                def pick(logits, top, code, one_hot):
                    ch.link(v.tensor_reduce(top[:, :], logits[:, :, :], AX_X, ALU.max))
                    ch.link(v.tensor_tensor(a1[:, :, :], logits[:, :, :], over_e(top[:, :]), ALU.is_equal))
                    ch.link(v.tensor_tensor(a1[:, :, :], a1[:, :, :], rev[:, :, :], ALU.mult))
                    ch.link(v.tensor_reduce(code[:, :], a1[:, :, :], AX_X, ALU.max))
                    ch.link(v.tensor_tensor(one_hot[:, :, :], rev[:, :, :], over_e(code[:, :]), ALU.is_equal))

                dve.wait_ge(made, 8)
                pick(LG, m1, c1, first)
                ch.link(v.scalar_tensor_tensor(out=a2[:, :, :], in0=first[:, :, :], scalar=-HUGE, in1=LG[:, :, :],
                                               op0=ALU.mult, op1=ALU.add))
                pick(a2, m2, c1, second)
                ch.link(v.tensor_tensor(both[:, :, :], first[:, :, :], second[:, :, :], ALU.add))
                assert ch.n == ROUTE_BOTH
                v.tensor_tensor(dl[:, :], m2[:, :], m1[:, :], ALU.subtract).then_inc(gap, 1)
                dve.wait_ge(counted, 2)
                ch.link(v.tensor_copy(tile_n[:, :, :], PS[:, 1, 0:T * E].rearrange("p (t e) -> p e t", e=E)))
                flat_n, flat_i, flat_x = (a[:, :, :].rearrange("p e t -> p (e t)") for a in (tile_n, incl, excl))
                ch.link(v.tensor_tensor_scan(flat_i, one8[:, :], flat_n, 0.0, ALU.mult, ALU.add))
                ch.link(v.tensor_tensor(flat_x, flat_i, flat_n, ALU.subtract))
                ch.link(v.tensor_tensor(tot[:, :], incl[:, :, T - 1], excl[:, :, 0], ALU.subtract))
                ch.link(v.tensor_tensor(incl[:, :, :], over_t(tot[:, :]), edge[:, :, :], ALU.is_gt))
                ch.link(v.tensor_reduce(nblk[:, :], incl[:, :, :], AX_X, ALU.add))
                ch.link(v.tensor_tensor_scan(bend[:, :], one8[:, 0:E], nblk[:, :], 0.0, ALU.mult, ALU.add))
                ch.link(v.tensor_tensor(base[:, :], bend[:, :], nblk[:, :], ALU.subtract))
                ch.link(v.scalar_tensor_tensor(out=base[:, :], in0=base[:, :], scalar=float(P), in1=excl[:, :, 0],
                                               op0=ALU.mult, op1=ALU.subtract))
                ch.link(v.tensor_tensor(incl[:, :, :], excl[:, :, :], over_t(base[:, :]), ALU.add))
                ch.link(v.tensor_tensor(a1[:, :, :], PS[:, 0, 0:T * E].rearrange("p (t e) -> p t e", e=E),
                                        incl[:, :, :].rearrange("p e t -> p t e"), ALU.add))
                for k, hot_k in enumerate((first, second)):
                    ch.link(v.tensor_tensor(a2[:, :, :], hot_k[:, :, :], a1[:, :, :], ALU.mult))
                    ch.link(v.tensor_reduce(pos[:, :, k], a2[:, :, :], AX_X, ALU.add))
                flat_pos = pos[:, :, :].rearrange("p t k -> p (t k)")
                ch.post(v.tensor_copy(ye_idx[:, :, :], pos[:, :, :]))
                ch.link(v.tensor_copy(posi[:, :], flat_pos))
                ch.link(v.tensor_scalar(part[:, :], posi[:, :], P - 1, None, ALU.bitwise_and))
                ch.link(v.tensor_copy(low[:, :], part[:, :]))
                ch.link(v.tensor_scalar(part[:, :], posi[:, :], 7, None, ALU.logical_shift_right))
                ch.link(v.tensor_copy(high[:, :], part[:, :]))

                def heat(n, u):
                    after(dve, placed, n - (Q - 1))
                    dve.wait_ge(dch, ROUTE_PLACES)
                    at = bass.ds(n, 1)
                    v.tensor_scalar(lo_hot[:, u, :], col[:, :], low[:, at],
                                    tok[:, :, :].rearrange("p t k -> p (t k)")[:, at],
                                    ALU.is_equal, ALU.mult).then_inc(hot, 1)
                    v.tensor_scalar(hi_hot[:, u, :], col[:, 0:NBE], high[:, at], None, ALU.is_equal).then_inc(hot, 1)

                assert ch.n == ROUTE_PLACES
                for u in range(Q):
                    heat(u, u)
                with dve.Fori(1, 2 * T // Q) as i:
                    for u in range(Q):
                        heat(Q * i + u, u)
                ch.link(v.tensor_tensor(b1_[:, :, :], jid[:, :, :],
                                        bend[:, :].unsqueeze(1).broadcast_to([P, NBE, E]), ALU.is_ge))
                ch.link(v.tensor_reduce(be[:, :], b1_[:, :, :], AX_X, ALU.add))
                ch.link(v.tensor_scalar(be[:, :], be[:, :], float(E - 1), None, ALU.min))
                ch.post(v.tensor_copy(blk_exp[:, :], be[:, :]))
                ch.link(v.tensor_tensor(b1_[:, :, :], eid[:, :, :],
                                        be[:, :].unsqueeze(2).broadcast_to([P, NBE, E]), ALU.is_equal))
                ch.link(v.tensor_tensor(b2_[:, :, :], b1_[:, :, :],
                                        winv[:, :].unsqueeze(1).broadcast_to([P, NBE, E]), ALU.mult))
                ch.link(v.tensor_reduce(blk_inv[:, :], b2_[:, :, :], AX_X, ALU.add))
                dve.wait_ge(exped, 1)
                ch.link(v.tensor_scalar(r2[:, :], e2[:, :], 1.0, None, ALU.add))
                ch.link(v.reciprocal(prob[:, 0, :], r2[:, :]))
                ch.link(v.tensor_tensor(prob[:, 1, :], e2[:, :], prob[:, 0, :], ALU.mult))
                dve.wait_ge(placed, 2 * T)
                ch.link(v.tensor_copy(tok_idx[:, :], PS[:, 2, 0:NBE]))


ROUTE_BOTH = 12
ROUTE_PLACES = ROUTE_BOTH + 21


def experts(nc, sem, PS, ident, W12H, W12L, W3H, W3L, blk_inv, blk_exp, tok_idx, z_dram, yd):
    st = ExitStack()
    with st:
        def sb(name, shape, dt=F32):
            return st.enter_context(nc.sbuf_tensor(name, shape, dt))

        idx = sb("block_tokens", [P, 2], U32)
        zg = sb("z_gathered", [P, 2, D])
        zh = sb("zT_high", [P, 2, DC * P], F16)
        zl = sb("zT_low", [P, 2, DC * P], F16)
        s = sb("silu", [P, 2, H])
        g = sb("hidden", [P, 2, H])
        gh = sb("hiddenT_high", [P, HC * P], F32R)
        gl = sb("hiddenT_low", [P, HC * P], F32R)
        ye = sb("expert_out", [P, 2, D])

        z_in = [sem("z_gathered0"), sem("z_gathered1")]
        ye_out = [sem("ye_out0"), sem("ye_out1")]
        idx_made = sem("idx_made")
        zt_made, zh_made, zl_made, h1_made, h2_made, s_made, g_made = (sem("moe_" + n) for n in (
            "zt", "zt_high", "zt_low", "h1", "h2", "silu", "hidden"))
        gt_made, gh_made, gl_made, y_made, ye_made = (sem("moe_" + n) for n in (
            "hidden_t", "hidden_high", "hidden_low", "y", "ye"))
        PAIRS = (NB - 3) // 2
        REST = range(2 * PAIRS, NB)

        def steps(eng, first, step):
            first()
            for j in range(2):
                step(j, j, 0, True, True)
            with eng.Fori(1, PAIRS) as i:
                for u in range(2):
                    step(2 * i + u, u, 2 * i, True, True)
            for j in REST:
                step(j, j % 2, j - j % 2, j + 1 < NB, j + 2 < NB)

        with nc.Block() as block:
            @block.gpsimd
            def _(pool):
                def gather(j, u, i2):
                    after(pool, z_in[u], 8 * i2)
                    pool.tensor_copy(idx[:, u:u + 1], tok_idx[:, bass.ds(j, 1)]).then_inc(idx_made, 1)
                    after(pool, zt_made, i2)
                    apart(pool, idx_made, j + 1)
                    pool.indirect_dma_start(zg[:, u, :], None, z_dram[:, :],
                                            bass.IndirectOffsetOnAxis(ap=idx[:, u:u + 1], axis=0)).then_inc(z_in[u], 16)

                for j in range(2):
                    gather(j, j, 0)
                with pool.Fori(1, NB // 2) as i:
                    for u in range(2):
                        gather(2 * i + u, u, 2 * i)
                gather(NB - 1, 0, NB - 1)

            @block.sync
            def _(sp):
                def store(j, u):
                    sp.wait_ge(ye_made, j + 1)
                    sp.dma_start(yd[:, bass.ds(j, 1), :], ye[:, u, :]).then_inc(ye_out[u], 16)

                with sp.Fori(0, NB // 2) as i:
                    for u in range(2):
                        store(2 * i + u, u)
                store(NB - 1, 0)
                sp.wait_ge(ye_out[0], 16 * (NB // 2 + 1))
                sp.wait_ge(ye_out[1], 16 * (NB // 2))

            @block.tensor
            def _(pe):
                def turn_z(j, u, i2):
                    after(pe, zl_made, j)
                    pe.wait_ge(z_in[u], 8 * i2 + 16)
                    for c in range(DC):
                        mm = pe.transpose(PS[:, 0, c * P:(c + 1) * P], zg[:, u, c * P:(c + 1) * P], ident[:, :])
                    mm.then_inc(zt_made, 1)

                def up(j, u):
                    e = bass.ds(pe.value_load(blk_exp[0:1, bass.ds(j, 1)], min_val=0, max_val=E - 1), 1)
                    pe.wait_ge(zl_made, j + 1)
                    for half, freed, made in ((0, s_made, h1_made), (1, g_made, h2_made)):
                        after(pe, freed, j - 1)
                        n = 0
                        for c in range(DC):
                            for zz, w in ((zh, W12L), (zh, W12H), (zl, W12H)):
                                mm = pe.matmul(PS[:, 1 + half + 2 * u, :], zz[:, u, c * P:(c + 1) * P],
                                               w[:, e, c, half * H:(half + 1) * H].rearrange("p a h -> p (a h)"),
                                               start=(n == 0), stop=(n == 3 * DC - 1))
                                n += 1
                        mm.then_inc(made, 1)

                def turn_g(j, u):
                    after(pe, gl_made, j)
                    pe.wait_ge(g_made, j + 1)
                    for c in range(HC):
                        mm = pe.transpose(PS[:, 5, c * P:(c + 1) * P], g[:, u, c * P:(c + 1) * P], ident[:, :])
                    mm.then_inc(gt_made, 1)

                def down(j, u, i2):
                    e = bass.ds(pe.value_load(blk_exp[0:1, bass.ds(j, 1)], min_val=0, max_val=E - 1), 1)
                    pe.wait_ge(gl_made, j + 1)
                    after(pe, ye_made, i2)
                    n = 0
                    for c in range(HC):
                        for gg, w in ((gh, W3L), (gh, W3H), (gl, W3H)):
                            mm = pe.matmul(PS[:, 6 + u, 0:D], gg[:, c * P:(c + 1) * P],
                                           w[:, e, c, :].rearrange("p a d -> p (a d)"),
                                           start=(n == 0), stop=(n == 3 * HC - 1))
                            n += 1
                    mm.then_inc(y_made, 1)

                def first():
                    turn_z(0, 0, 0)
                    up(0, 0)
                    turn_z(1, 1, 0)

                def step(j, u, i2, more, more2):
                    turn_g(j, u)
                    if more:
                        up(j + 1, 1 - u)
                    if more2:
                        turn_z(j + 2, u, i2 + 2)
                    down(j, u, i2)

                steps(pe, first, step)

            @block.scalar
            def _(act):
                a = nc.scalar

                def part_z(j, u):
                    after(act, h2_made, j - 1)
                    act.wait_ge(zt_made, j + 1)
                    a.activation(zh[:, u, :], PS[:, 0, 0:D], ACT.Copy).then_inc(zh_made, 1)

                def silu(j, u):
                    act.wait_ge(h1_made, 1)
                    after(act, g_made, j - 1)
                    act.wait_ge(h1_made, j + 1)
                    a.activation(s[:, u, :], PS[:, 1 + 2 * u, :], ACT.Silu, scale=blk_inv[:, bass.ds(j, 1)])\
                        .then_inc(s_made, 1)

                def part_g(j, u):
                    act.wait_ge(gt_made, j + 1)
                    a.activation(gh[:, :], PS[:, 5, :], ACT.Copy).then_inc(gh_made, 1)

                def keep_y(j, u, i2):
                    after(act, ye_out[u], 8 * i2)
                    act.wait_ge(y_made, j + 1)
                    a.activation(ye[:, u, :], PS[:, 6 + u, 0:D], ACT.Copy).then_inc(ye_made, 1)

                def first():
                    part_z(0, 0)
                    silu(0, 0)
                    part_z(1, 1)

                def step(j, u, i2, more, more2):
                    part_g(j, u)
                    if more:
                        silu(j + 1, 1 - u)
                    if more2:
                        part_z(j + 2, u)
                    keep_y(j, u, i2)

                steps(act, first, step)

            @block.vector
            def _(dve):
                v = nc.vector

                def part_z(j, u):
                    after(dve, h2_made, j - 1)
                    dve.wait_ge(zh_made, j + 1)
                    v.tensor_tensor(zl[:, u, :], PS[:, 0, 0:D], zh[:, u, :], ALU.subtract).then_inc(zl_made, 1)

                def hidden(j, u):
                    after(dve, gt_made, j - 1)
                    dve.wait_ge(s_made, j + 1)
                    dve.wait_ge(h2_made, j + 1)
                    v.scalar_tensor_tensor(out=g[:, u, :], in0=PS[:, 2 + 2 * u, :], scalar=blk_inv[:, bass.ds(j, 1)],
                                           in1=s[:, u, :], op0=ALU.mult, op1=ALU.mult).then_inc(g_made, 1)

                def part_g(j, u):
                    dve.wait_ge(gh_made, j + 1)
                    v.tensor_tensor(gl[:, :], PS[:, 5, :], gh[:, :].bitcast(F32), ALU.subtract).then_inc(gl_made, 1)

                def first():
                    part_z(0, 0)
                    hidden(0, 0)
                    part_z(1, 1)

                def step(j, u, i2, more, more2):
                    part_g(j, u)
                    if more:
                        hidden(j + 1, 1 - u)
                    if more2:
                        part_z(j + 2, u)

                steps(dve, first, step)


def attend1(nc, sem, PS, X1, ident, rowmask, prob, ye_idx, ye_dram, cd):
    st = ExitStack()
    with st:
        def sb(name, shape, dt=F32):
            return st.enter_context(nc.sbuf_tensor(name, shape, dt))

        cs = sb("c1_in", [P, Q, D])
        idx = sb("row_places", [P, Q, 2], U32)
        rows = sb("expert_rows_in", [P, Q, 2, D])
        cT = sb("c1_T", [P, 2, DC * P])
        qT = sb("q_T", [P, 2, DC * P])
        qs = sb("q_neg", [P, Q, D])
        ne = sb("neg_scores", [P, Q, P])
        least = sb("neg_max", [P, Q])
        pr = sb("exps", [P, Q, P])
        pT = sb("exps_T", [P, Q, P])
        total = sb("exp_sums", [P, Q])
        inv = sb("exp_invs", [P, Q])
        stt = sb("moments1_in", [P, Q, 6])
        mean, var, rst, tmp, qsc, qbi = (sb(n, [P, Q]) for n in (
            "means1", "vars1", "rstds1", "tmp1", "q_scales", "q_biases"))

        c_in = [sem(f"c1_in{k}") for k in range(Q)]
        r_in = [[sem(f"rows_in{k}{n}") for n in range(2)] for k in range(Q)]
        idx_made, x2_half, x2_made, x2_stat, norms_made, q_made = (sem("a1_" + n) for n in (
            "idx", "x2_half", "x2", "x2_stat", "norms", "q"))
        ct_made, ct_kept, qt_made, qt_kept, sc_made, ne_made, p_made = (sem("a1_" + n) for n in (
            "ct_made", "ct_kept", "qt_made", "qt_kept", "scores", "neg_scores", "exps"))
        pt_made, pt_kept, inv_made, o_made, x3_made = (sem("a1_" + n) for n in (
            "pt_made", "pt_kept", "inverse", "out", "x3"))
        LINKS = NORM_N + 2

        def at(i, k):
            return bass.ds(Q * i + k, 1)

        def x_row(i, k):
            return X1[:, at(i, k), :].rearrange("p a d -> p (a d)")

        with nc.Block() as block:
            @block.sync
            def _(sp):
                def load(i, k):
                    after(sp, o_made, Q * i + (k - 3))
                    sp.dma_start(cs[:, k, :], cd[:, at(i, k), :]).then_inc(c_in[k], 16)

                for k in range(Q):
                    load(0, k)
                with sp.Fori(1, NQ) as i:
                    for k in range(Q):
                        load(i, k)

            @block.gpsimd
            def _(pool):
                def gathers(i):
                    for k in range(Q):
                        for n in range(2):
                            after(pool, r_in[k][n], 16 * i)
                    apart(pool, r_in[0][0], 16 * i)
                    pool.tensor_copy(idx[:, :, :], ye_idx[:, bass.ds(Q * i, Q), :]).then_inc(idx_made, 1)
                    pool.wait_ge(idx_made, i + 1)
                    for k in range(Q):
                        apart(pool, x2_made, Q * i + (k - 3))
                        for n in range(2):
                            pool.indirect_dma_start(rows[:, k, n, :], None, ye_dram[:, :],
                                                    bass.IndirectOffsetOnAxis(ap=idx[:, k, n:n + 1], axis=0))\
                                .then_inc(r_in[k][n], 16)

                gathers(0)
                with pool.Fori(1, NQ) as i:
                    gathers(i)

            @block.scalar
            def _(act):
                a = nc.scalar

                def keep_turned(i, k):
                    after(act, sc_made, Q * i + (k - 1))
                    act.wait_ge(ct_made, Q * i + (k + 1))
                    a.activation(cT[:, k % 2, :], PS[:, k % 2, 0:D], ACT.Copy).then_inc(ct_kept, 1)
                    act.wait_ge(qt_made, Q * i + (k + 1))
                    a.activation(qT[:, k % 2, :], PS[:, 2, 0:D], ACT.Copy).then_inc(qt_kept, 1)

                def exps(i, k):
                    after(act, pt_made, Q * i + (k - 3))
                    act.wait_ge(ne_made, Q * i + (k + 1))
                    if k == 0:
                        after(act, inv_made, i)
                    a.activation(pr[:, k, :], ne[:, k, :], ACT.Exp, scale=-1.0, bias=least[:, k:k + 1],
                                 accum_out=total[:, k:k + 1]).then_inc(p_made, 1)

                def keep_pt(i, k):
                    after(act, o_made, Q * i + (k - 3))
                    act.wait_ge(pt_made, Q * i + (k + 1))
                    a.activation(pT[:, k, :], PS[:, 4 + k % 2, 0:P], ACT.Copy).then_inc(pt_kept, 1)

                def make_q(i, k):
                    act.wait_ge(norms_made, 1)
                    act.wait_ge(norms_made, LINKS * i + LINKS)
                    after(act, qt_made, Q * i + (k - 3))
                    a.activation(qs[:, k, :], x_row(i, k), ACT.Identity, scale=qsc[:, k:k + 1],
                                 bias=qbi[:, k:k + 1]).then_inc(q_made, 1)

                def group(i, final=False):
                    for k in range(Q):
                        keep_turned(i, k)
                        if k >= 1:
                            exps(i, k - 1)
                    exps(i, Q - 1)
                    for k in range(Q):
                        keep_pt(i, k)
                    if not final:
                        for k in range(Q):
                            make_q(i + 1, k)

                for k in range(Q):
                    make_q(0, k)
                group(0)
                with act.Fori(1, NQ - 1) as i:
                    group(i)
                group(NQ - 1, final=True)

            @block.tensor
            def _(pe):
                def turn(i, k):
                    after(pe, ct_kept, Q * i + (k - 1))
                    pe.wait_ge(c_in[k], 16 * i + 16)
                    for c in range(DC):
                        mm = pe.transpose(PS[:, k % 2, c * P:(c + 1) * P], cs[:, k, c * P:(c + 1) * P], ident[:, :])
                    mm.then_inc(ct_made, 1)
                    after(pe, qt_kept, Q * i + k)
                    pe.wait_ge(q_made, Q * i + (k + 1))
                    for c in range(DC):
                        mm = pe.transpose(PS[:, 2, c * P:(c + 1) * P], qs[:, k, c * P:(c + 1) * P], ident[:, :])
                    mm.then_inc(qt_made, 1)

                def scores(i, k):
                    after(pe, ne_made, Q * i + k)
                    pe.wait_ge(ct_kept, Q * i + (k + 1))
                    pe.wait_ge(qt_kept, Q * i + (k + 1))
                    for c in range(DC):
                        mm = pe.matmul(PS[:, 3, 0:P], qT[:, k % 2, c * P:(c + 1) * P], cT[:, k % 2, c * P:(c + 1) * P],
                                       start=(c == 0), stop=(c == DC - 1))
                    mm.then_inc(sc_made, 1)

                def turn_p(i, k):
                    after(pe, pt_kept, Q * i + (k - 1))
                    pe.wait_ge(p_made, Q * i + (k + 1))
                    pe.transpose(PS[:, 4 + k % 2, 0:P], pr[:, k, :], ident[:, :]).then_inc(pt_made, 1)

                def product(i, k):
                    after(pe, x3_made, Q * i + (k - 1))
                    pe.wait_ge(pt_kept, Q * i + (k + 1))
                    pe.matmul(PS[:, 6 + k % 2, 0:D], pT[:, k, :], cs[:, k, :], start=True, stop=True)\
                        .then_inc(o_made, 1)

                def group(i):
                    for k in range(Q):
                        turn(i, k)
                        if k >= 1:
                            scores(i, k - 1)
                    scores(i, Q - 1)
                    for k in range(Q):
                        turn_p(i, k)
                    for k in range(Q):
                        product(i, k)

                group(0)
                with pe.Fori(1, NQ) as i:
                    group(i)

            @block.vector
            def _(dve):
                v = nc.vector

                def sum_rows(i, k):
                    dve.wait_ge(r_in[k][0], 16 * i + 16)
                    v.scalar_tensor_tensor(out=x_row(i, k), in0=rows[:, k, 0, :], scalar=prob[:, 0, at(i, k)],
                                           in1=x_row(i, k), op0=ALU.mult, op1=ALU.add).then_inc(x2_half, 1)

                def sum_rows2(i, k):
                    dve.wait_ge(r_in[k][1], 16 * i + 16)
                    dve.wait_ge(x2_half, Q * i + (k + 1))
                    v.scalar_tensor_tensor(out=x_row(i, k), in0=rows[:, k, 1, :], scalar=prob[:, 1, at(i, k)],
                                           in1=x_row(i, k), op0=ALU.mult, op1=ALU.add).then_inc(x2_made, 1)

                def moments_x(i, k):
                    apart(dve, x2_made, Q * i + (k + 1))
                    v.bn_stats(stt[:, k, :], x_row(i, k)).then_inc(x2_stat, 1)

                def norms(i):
                    dve.wait_ge(x2_stat, Q * i + Q)
                    after(dve, q_made, Q * i)
                    ch = Chain(dve, norms_made, LINKS * i)
                    moments(v, ch, stt[:, :, :], mean[:, :], var[:, :], tmp[:, :])
                    ch.link(v.tensor_scalar(var[:, :], var[:, :], LN_EPS, None, ALU.add))
                    rsqrt_steps(v, ch, rst[:, :], var[:, :], tmp[:, :])
                    ch.link(v.tensor_scalar(qsc[:, :], rst[:, :], -1.0 / 16.0, None, ALU.mult))
                    ch.link(v.scalar_tensor_tensor(out=qbi[:, :], in0=mean[:, :], scalar=-1.0, in1=qsc[:, :],
                                                   op0=ALU.mult, op1=ALU.mult))
                    assert ch.n == LINKS

                def front(i):
                    for k in range(Q):
                        sum_rows(i, k)
                        if k >= 1:
                            sum_rows2(i, k - 1)
                        if k >= 2:
                            moments_x(i, k - 2)
                    sum_rows2(i, Q - 1)
                    moments_x(i, Q - 2)
                    moments_x(i, Q - 1)

                def masked(i, k):
                    after(dve, p_made, Q * i + (k - 3))
                    dve.wait_ge(sc_made, Q * i + (k + 1))
                    v.tensor_scalar(ne[:, k, :], PS[:, 3, 0:P], rowmask[:, at(i, k)], HUGE, ALU.add, ALU.min,
                                    accum_out=least[:, k:k + 1]).then_inc(ne_made, 1)

                def add_out(i, k):
                    dve.wait_ge(o_made, Q * i + (k + 1))
                    dve.wait_ge(inv_made, i + 1)
                    v.scalar_tensor_tensor(out=x_row(i, k), in0=PS[:, 6 + k % 2, 0:D], scalar=inv[:, k:k + 1],
                                           in1=x_row(i, k), op0=ALU.mult, op1=ALU.add).then_inc(x3_made, 1)

                def group(i, final=False):
                    for k in range(Q):
                        masked(i, k)
                    if not final:
                        front(i + 1)
                    dve.wait_ge(p_made, Q * i + Q)
                    after(dve, x3_made, Q * i)
                    v.reciprocal(inv[:, :], total[:, :]).then_inc(inv_made, 1)
                    for k in range(Q):
                        add_out(i, k)
                    if not final:
                        norms(i + 1)

                front(0)
                norms(0)
                group(0)
                with dve.Fori(1, NQ - 1) as i:
                    group(i)
                group(NQ - 1, final=True)


def bitffn(nc, sem, PS, X1, ident, magic, wmean, w1q, w2q, b1b, b2b, od):
    st = ExitStack()
    with st:
        def sb(name, shape, dt=F32):
            return st.enter_context(nc.sbuf_tensor(name, shape, dt))

        d = sb("x_centred", [P, Q, D])
        xb = sb("x_plus_b2", [P, Q, D])
        t1 = sb("x_rounded", [P, Q, D])
        x1T = sb("x_whole_T", [P, 2, DC * P], BF16)
        h = sb("hidden_ffn", [P, Q, F])
        junk = sb("squares", [P, F])
        t2 = sb("h_rounded", [P, Q, F])
        hT = sb("h_whole_T", [P, 2, FC * P], BF16)
        fin = sb("rows_out", [P, Q, D])
        stt = sb("moments2_in", [P, Q, 6])
        (mean, var, rst, tmp, am, a1, k1, al, ss, am2, r2, v2, tm2, a2, k2, be) = (sb("ffn_" + n, [P, Q]) for n in (
            "mean", "var", "rst", "tmp", "amax", "clip", "k1", "alpha", "squares", "amax2", "rst2", "var2", "tmp2",
            "clip2", "k2", "beta"))
        wm = sb("ffn_wmean", [P, 2])

        x_stat, norm_links, d_made, xb_made, am_made, t1_made = (sem("f_" + n) for n in (
            "x_stat", "norm_links", "centred", "x_b2", "amax", "x_rounded"))
        xt_made, xt_kept, h_made, u_made, gelu_made, sq_made, am2_made = (sem("f_" + n) for n in (
            "xt_made", "xt_kept", "h_psum", "h_biased", "gelu", "squares", "amax2"))
        links2, t2_made, ht_made, ht_kept, y_made, fin_made = (sem("f_" + n) for n in (
            "links2", "h_rounded", "ht_made", "ht_kept", "y_psum", "final"))
        o_out = [sem(f"out_stored{k}") for k in range(Q)]
        wm_made = sem("f_wmean")
        L1A = MOMENTS_N + 1 + RSQRT_N
        L1 = L1A + 5
        L2 = 1 + RSQRT_N + 5

        def at(i, k):
            return bass.ds(Q * i + k, 1)

        def x_row(i, k):
            return X1[:, at(i, k), :].rearrange("p a d -> p (a d)")

        with nc.Block() as block:
            @block.sync
            def _(sp):
                def store(i, k):
                    sp.wait_ge(fin_made, Q * i + (k + 1))
                    sp.dma_start(od[:, at(i, k), :], fin[:, k, :]).then_inc(o_out[k], 16)

                with sp.Fori(0, NQ) as i:
                    for k in range(Q):
                        store(i, k)
                for k in range(Q):
                    sp.wait_ge(o_out[k], 16 * NQ)

            @block.gpsimd
            def _(pool):
                def centre(i, k):
                    after(pool, t1_made, Q * i + (k - 3))
                    pool.wait_ge(norm_links, 1)
                    pool.wait_ge(norm_links, L1 * i + L1A)
                    pool.tensor_tensor(d[:, k, :], x_row(i, k), mean[:, k:k + 1].broadcast_to([P, D]), ALU.subtract)\
                        .then_inc(d_made, 1)

                def add_b2(i, k):
                    pool.wait_ge(d_made, 1)
                    after(pool, fin_made, Q * i + (k - 3))
                    pool.tensor_tensor(xb[:, k, :], x_row(i, k), b2b[:, :], ALU.add).then_inc(xb_made, 1)

                for k in range(Q):
                    centre(0, k)
                def group(i):
                    for k in range(Q):
                        add_b2(i, k)
                    for k in range(Q):
                        centre(i + 1, k)

                group(0)
                with pool.Fori(1, NQ - 1) as i:
                    group(i)
                for k in range(Q):
                    add_b2(NQ - 1, k)

            @block.scalar
            def _(act):
                a = nc.scalar

                def round_x(i, k):
                    after(act, xt_made, Q * i + (k - 3))
                    act.wait_ge(norm_links, L1 * i + L1)
                    a.activation(t1[:, k, :], d[:, k, :], ACT.Identity, scale=k1[:, k:k + 1], bias=magic[:, 0:1])\
                        .then_inc(t1_made, 1)

                def keep_xt(i, k):
                    after(act, h_made, Q * i + (k - 1))
                    act.wait_ge(xt_made, Q * i + (k + 1))
                    a.activation(x1T[:, k % 2, :], PS[:, 0, 0:D], ACT.Identity, bias=magic[:, 1:2]).then_inc(xt_kept, 1)

                def gelu(i, k):
                    act.wait_ge(u_made, Q * i + (k + 1))
                    a.activation(h[:, k, :], h[:, k, :], ACT.Gelu).then_inc(gelu_made, 1)

                def square(i, k):
                    act.wait_ge(gelu_made, Q * i + (k + 1))
                    after(act, sq_made, Q * i + k)
                    if k == 0:
                        after(act, links2, L2 * i)
                    a.activation(junk[:, :], h[:, k, :], ACT.Square, accum_out=ss[:, k:k + 1]).then_inc(sq_made, 1)

                def keep_ht(i, k):
                    after(act, y_made, Q * i + (k - 1))
                    act.wait_ge(ht_made, Q * i + (k + 1))
                    a.activation(hT[:, k % 2, :], PS[:, 3:5, :].rearrange("p a b -> p (a b)"), ACT.Identity,
                                 bias=magic[:, 1:2]).then_inc(ht_kept, 1)

                def group(i, before, here=True):
                    if here:
                        for k in range(Q):
                            round_x(i, k)
                    for k in range(Q):
                        if here:
                            keep_xt(i, k)
                        if before:
                            keep_ht(i - 1, k)
                        if here:
                            if k >= 1:
                                square(i, k - 1)
                            gelu(i, k)
                    if here:
                        square(i, Q - 1)

                group(0, False)
                group(1, True)
                with act.Fori(2, NQ) as i:
                    group(i, True)
                group(NQ, True, False)

            @block.tensor
            def _(pe):
                def turn_x(i, k):
                    after(pe, xt_kept, Q * i + k)
                    pe.wait_ge(t1_made, Q * i + (k + 1))
                    for c in range(DC):
                        mm = pe.transpose(PS[:, 0, c * P:(c + 1) * P], t1[:, k, c * P:(c + 1) * P], ident[:, :])
                    mm.then_inc(xt_made, 1)

                def up(i, k):
                    after(pe, u_made, Q * i + k)
                    pe.wait_ge(xt_kept, Q * i + (k + 1))
                    for c in range(DC):
                        for half in range(2):
                            mm = pe.matmul(PS[:, 1 + half, :], x1T[:, k % 2, c * P:(c + 1) * P],
                                           w1q[:, c, half * 512:(half + 1) * 512], start=(c == 0), stop=(c == DC - 1))
                    mm.then_inc(h_made, 1)

                def turn_h(i, k):
                    after(pe, ht_kept, Q * i + k)
                    pe.wait_ge(t2_made, Q * i + (k + 1))
                    for c in range(FC):
                        mm = pe.transpose(PS[:, 3 + c // 4, (c % 4) * P:(c % 4 + 1) * P],
                                          t2[:, k, c * P:(c + 1) * P], ident[:, :])
                    mm.then_inc(ht_made, 1)

                def down(i, k):
                    after(pe, fin_made, Q * i + (k - 1))
                    pe.wait_ge(ht_kept, Q * i + (k + 1))
                    for c in range(FC):
                        mm = pe.matmul(PS[:, 5 + k % 2, 0:D], hT[:, k % 2, c * P:(c + 1) * P], w2q[:, c, :],
                                       start=(c == 0), stop=(c == FC - 1))
                    mm.then_inc(y_made, 1)

                def group(i, before, here=True):
                    for k in range(Q):
                        if here:
                            turn_x(i, k)
                        if before:
                            turn_h(i - 1, k)
                        if here:
                            up(i, k)
                        if before:
                            down(i - 1, k)

                group(0, False)
                group(1, True)
                with pe.Fori(2, NQ) as i:
                    group(i, True)
                group(NQ, True, False)

            @block.vector
            def _(dve):
                v = nc.vector

                def moments_x(i, k):
                    v.bn_stats(stt[:, k, :], x_row(i, k)).then_inc(x_stat, 1)

                def norms(i):
                    dve.wait_ge(x_stat, Q * i + Q)
                    after(dve, d_made, Q * i)
                    ch = Chain(dve, norm_links, L1 * i)
                    moments(v, ch, stt[:, :, :], mean[:, :], var[:, :], tmp[:, :])
                    ch.link(v.tensor_scalar(var[:, :], var[:, :], 1.0 + RMS_EPS, RMS_EPS * LN_EPS, ALU.mult, ALU.add))
                    rsqrt_steps(v, ch, rst[:, :], var[:, :], tmp[:, :])
                    assert ch.n == L1A

                def largest_x(i, k):
                    dve.wait_ge(d_made, Q * i + (k + 1))
                    v.tensor_reduce(am[:, k:k + 1], d[:, k, :], AX_X, ALU.max, apply_absolute_value=True)\
                        .then_inc(am_made, 1)

                def scale_x(i):
                    dve.wait_ge(am_made, Q * i + Q)
                    after(dve, u_made, Q * i)
                    after(dve, t1_made, Q * i)
                    ch = Chain(dve, norm_links, L1 * i + L1A)
                    ch.link(v.tensor_tensor(a1[:, :], am[:, :], rst[:, :], ALU.mult))
                    ch.link(v.tensor_scalar(a1[:, :], a1[:, :], QUANT_EPS, 1.0 / 127.0, ALU.max, ALU.mult))
                    ch.post(v.tensor_scalar(al[:, :], a1[:, :], wm[:, 0:1], None, ALU.mult))
                    ch.link(v.reciprocal(k1[:, :], a1[:, :]))
                    ch.link(v.tensor_tensor(k1[:, :], k1[:, :], rst[:, :], ALU.mult))
                    assert ch.n == L1 - L1A

                def bias_h(i, k):
                    after(dve, t2_made, Q * i + (k - 3))
                    dve.wait_ge(h_made, Q * i + (k + 1))
                    v.scalar_tensor_tensor(out=h[:, k, :], in0=PS[:, 1:3, :].rearrange("p a b -> p (a b)"),
                                           scalar=al[:, k:k + 1], in1=b1b[:, :], op0=ALU.mult, op1=ALU.add)\
                        .then_inc(u_made, 1)

                def largest_h(i, k):
                    dve.wait_ge(gelu_made, Q * i + (k + 1))
                    v.tensor_reduce(am2[:, k:k + 1], h[:, k, :], AX_X, ALU.max, apply_absolute_value=True)\
                        .then_inc(am2_made, 1)

                def scale_h(i):
                    dve.wait_ge(am2_made, Q * i + Q)
                    dve.wait_ge(sq_made, Q * i + Q)
                    after(dve, fin_made, Q * i)
                    ch = Chain(dve, links2, L2 * i)
                    ch.link(v.tensor_scalar(v2[:, :], ss[:, :], 1.0 / F, RMS_EPS, ALU.mult, ALU.add))
                    rsqrt_steps(v, ch, r2[:, :], v2[:, :], tm2[:, :])
                    ch.link(v.tensor_tensor(a2[:, :], am2[:, :], r2[:, :], ALU.mult))
                    ch.link(v.tensor_scalar(a2[:, :], a2[:, :], QUANT_EPS, 1.0 / 127.0, ALU.max, ALU.mult))
                    ch.post(v.tensor_scalar(be[:, :], a2[:, :], wm[:, 1:2], None, ALU.mult))
                    ch.link(v.reciprocal(k2[:, :], a2[:, :]))
                    ch.link(v.tensor_tensor(k2[:, :], k2[:, :], r2[:, :], ALU.mult))
                    assert ch.n == L2

                def round_h(i, k):
                    after(dve, ht_made, Q * i + (k - 3))
                    dve.wait_ge(links2, L2 * i + L2)
                    v.tensor_scalar(t2[:, k, :], h[:, k, :], k2[:, k:k + 1], ROUND, ALU.mult, ALU.add)\
                        .then_inc(t2_made, 1)

                def finish(i, k):
                    after(dve, o_out[k], 16 * i)
                    dve.wait_ge(xb_made, Q * i + (k + 1))
                    dve.wait_ge(y_made, Q * i + (k + 1))
                    v.scalar_tensor_tensor(out=fin[:, k, :], in0=PS[:, 5 + k % 2, 0:D], scalar=be[:, k:k + 1],
                                           in1=xb[:, k, :], op0=ALU.mult, op1=ALU.add).then_inc(fin_made, 1)

                def group(i, before, here=True, more=True):
                    for k in range(Q):
                        if before:
                            if k == 0:
                                round_h(i - 1, 0)
                            if k < Q - 1:
                                round_h(i - 1, k + 1)
                        if here:
                            bias_h(i, k)
                        if before:
                            finish(i - 1, k)
                        if here and k >= 1:
                            largest_h(i, k - 1)
                    if here:
                        if more:
                            for k in range(Q):
                                moments_x(i + 1, k)
                        largest_h(i, Q - 1)
                        if more:
                            norms(i + 1)
                        scale_h(i)
                        if more:
                            for k in range(Q):
                                largest_x(i + 1, k)
                            scale_x(i + 1)

                v.tensor_copy(wm[:, :], wmean[:, :]).then_inc(wm_made, 1)
                for k in range(Q):
                    moments_x(0, k)
                dve.wait_ge(wm_made, 1)
                norms(0)
                for k in range(Q):
                    largest_x(0, k)
                scale_x(0)
                group(0, False)
                group(1, True)
                with dve.Fori(2, NQ - 1) as i:
                    group(i, True)
                group(NQ - 1, True, True, False)
                group(NQ, True, False)


_INS = ['x', 'ctx_1024', 'mask_BxS_bk1', 'L0_ffn_w12', 'L0_ffn_w3', 'L0_ffn_gate_w', 'L1_ffn_w1', 'L1_ffn_b1',
        'L1_ffn_w2', 'L1_ffn_b2']


def kernel(**inputs):
    import numpy as np
    import concourse.bacc as bacc
    from concourse.bass_utils import run_bass_kernel_spmd

    nc = bacc.Bacc("TRN2", target_bir_lowering=False, num_devices=1)
    arrays, args = {}, []
    for name in _INS:
        a = np.ascontiguousarray(inputs[name])
        arrays[f"in_{name}"] = a
        args.append(nc.dram_tensor(f"in_{name}", a.shape, mybir.dt.from_np(a.dtype), kind="ExternalInput").ap())
    out = nc.dram_tensor("out", (T, P, D), F32, kind="ExternalOutput").ap()
    build(nc, *args, out)
    r = run_bass_kernel_spmd(nc, [arrays], core_ids=[0])
    return r.results[0]["out"]
```

```python
from contextlib import ExitStack

import concourse.bass as bass
from concourse import mybir

ALU = mybir.AluOpType
ACT = mybir.ActivationFunctionType
DT = mybir.dt
F32, F32R, F16, BF16 = DT.float32, DT.float32r, DT.float16, DT.bfloat16
I32, U32, U8 = DT.int32, DT.uint32, DT.uint8
AX_X = mybir.AxisListType.X

P = 128
T = 32
D = 256
DC = D // P
E = 8
H = 512
HC = H // P
F = 1024
FC = F // P
Q = 4
NQ = T // Q
R = 2 * Q
NR = T // R
NB = 2 * T + E - 1
NBE = NB + 1
LN_EPS = 1e-5
RMS_EPS = 1e-6
QUANT_EPS = 1e-5
NEG_BIG = 1e9
Z_SCALE = 1024.0
ROUND = 1.5 * 2.0 ** 23
RSQRT_SEED = 0x5F3759DF
HUGE = 3e38


def after(eng, sem, count):
    if not (isinstance(count, int) and count <= 0):
        eng.wait_ge(sem, count)


def apart(eng, sem, count):
    if isinstance(count, int):
        after(eng, sem, count)
    else:
        eng.wait_ge(sem, count)
        eng.nop(nofuse=True)


class Chain:

    def __init__(self, eng, sem, start):
        self.eng, self.sem, self.start, self.n = eng, sem, start, 0

    def post(self, ins):
        ins.then_inc(self.sem, 1)
        self.n += 1

    def join(self):
        self.eng.wait_ge(self.sem, self.start + self.n)

    def link(self, ins):
        self.post(ins)
        self.join()



def advance(sequence, n):
    for _ in range(n):
        next(sequence, None)


def rsqrt_steps(dve, chain, y, v, u):
    chain.join()
    chain.post(dve.tensor_scalar(y.bitcast(I32), v.bitcast(I32), 1, None, ALU.logical_shift_right))
    yield
    chain.join()
    chain.post(dve.tensor_scalar(y.bitcast(I32), y.bitcast(I32), -1, RSQRT_SEED, ALU.mult, ALU.add))
    yield
    for _ in range(3):
        chain.join()
        chain.post(dve.tensor_tensor(u, y, y, ALU.mult))
        yield
        chain.join()
        chain.post(dve.scalar_tensor_tensor(out=u, in0=u, scalar=-0.5, in1=v, op0=ALU.mult, op1=ALU.mult))
        yield
        chain.join()
        chain.post(dve.scalar_tensor_tensor(out=y, in0=u, scalar=1.5, in1=y, op0=ALU.add, op1=ALU.mult))
        yield


RSQRT_N = 11


def moments(dve, chain, st, mean, var, a):
    chain.post(dve.tensor_tensor(mean, st[:, :, 1], st[:, :, 4], ALU.add))
    chain.post(dve.tensor_tensor(a, st[:, :, 1], st[:, :, 4], ALU.subtract))
    chain.post(dve.tensor_tensor(var, st[:, :, 2], st[:, :, 5], ALU.add))
    yield
    chain.join()
    chain.post(dve.tensor_scalar(mean, mean, 0.5, None, ALU.mult))
    chain.post(dve.tensor_scalar(var, var, 1.0 / D, None, ALU.mult))
    chain.post(dve.tensor_tensor(a, a, a, ALU.mult))
    yield
    chain.join()
    chain.post(dve.scalar_tensor_tensor(out=var, in0=a, scalar=0.25, in1=var, op0=ALU.mult, op1=ALU.add))
    yield


MOMENTS_N = 7
NORM_N = MOMENTS_N + 1 + RSQRT_N


def at_tile(step, i, k, behind):
    shift, kk = divmod(k - behind, R)
    ii = i + shift
    if not isinstance(ii, int) or 0 <= ii < NR:
        step(ii, kk)


def build(nc, x, ctx_1024, mask_BxS_bk1, L0_ffn_w12, L0_ffn_w3, L0_ffn_gate_w,
          L1_ffn_w1, L1_ffn_b1, L1_ffn_w2, L1_ffn_b2, out):
    z_dram = nc.dram_tensor("z_rows", (T * P, 2 * D), F16, kind="Internal").ap()
    ye_dram = nc.dram_tensor("expert_rows", (NB * P, D), F32, kind="Internal").ap()
    xd = x.rearrange("b p d -> p b d")
    cd = ctx_1024.rearrange("b p d -> p b d")
    zd = z_dram.rearrange("(b p) d -> p b d", p=P)
    yd = ye_dram.rearrange("(b p) d -> p b d", p=P)
    od = out.rearrange("b p d -> p b d")

    whole = ExitStack()
    with whole:
        def sbw(name, shape, dt):
            return whole.enter_context(nc.sbuf_tensor(name, shape, dt))

        def sem(name):
            return whole.enter_context(nc.semaphore(name))

        PS = whole.enter_context(nc.psum_tensor("banks", [P, 8, 512], F32))

        X1 = sbw("x_rows", [P, T, D], F32)
        ident = sbw("ident", [P, P], F32)
        ident16 = sbw("ident16", [P, P], F16)
        ones = sbw("ones", [P, P], F32)
        tri = sbw("tri", [P, P], F32)
        rowmask = sbw("rowmask", [P, T], F32)
        ye_idx = sbw("ye_idx", [P, T, 2], U32)
        prob = sbw("prob", [P, 2, T], F32)

        w1q = sbw("w1_ternary", [P, DC, F], BF16)
        w2q = sbw("w2_ternary", [P, FC, D], BF16)
        wmean = sbw("w_means", [P, 2], F32)
        magic = sbw("magic", [P, 2], F32)

        moe = ExitStack()
        whole.enter_context(moe)

        def sbm(name, shape, dt):
            return moe.enter_context(nc.sbuf_tensor(name, shape, dt))

        W12H = sbm("w12_high", [P, E, DC, 2 * H], F16)
        W12L = sbm("w12_low", [P, E, DC, 2 * H], F16)
        W3H = sbm("w3_high", [P, E, HC, D], F32R)
        W3L = sbm("w3_low", [P, E, HC, D], F32R)
        blk_inv = sbm("blk_inv", [P, NBE], F32)
        blk_exp = sbm("blk_exp", [P, NBE], I32)
        tok_idx = sbm("tok_idx", [P, NBE], U32)
        gT = sbm("gate_T", [P, DC, E], F32)
        LG = sbm("logits", [P, T, E], F32)
        wsc = sbm("w12_scale", [P, E], F32)
        winv = sbm("w12_unscale", [P, E], F32)

        attend0(nc, sem, PS, X1, ident, ident16, ones, tri, rowmask, wsc, winv, gT, LG, W12H, W12L, W3H, W3L,
                xd, cd, zd, mask_BxS_bk1, L0_ffn_gate_w, L0_ffn_w12, L0_ffn_w3)
        route(nc, sem, PS, ones, ident16, LG, winv, prob, ye_idx, tok_idx, blk_exp, blk_inv, wmean, magic, w1q, w2q,
              L1_ffn_w1, L1_ffn_w2)
        experts(nc, sem, PS, ident, ident16, W12H, W12L, W3H, W3L, blk_inv, blk_exp, tok_idx, z_dram, yd)
        moe.close()
        b3 = sbw("b1_parts", [P, F], F32R)
        b2b = sbw("b2_rows", [P, D], F32)
        st3 = sbw("x3_moments", [P, T, 6], F32)
        attend1(nc, sem, PS, X1, ident, rowmask, prob, ye_idx, ye_dram, st3, cd, b3, b2b, L1_ffn_b1, L1_ffn_b2)
        bitffn(nc, sem, PS, X1, ident, magic, wmean, w1q, w2q, b3, b2b, st3, od)


def attend0(nc, sem, PS, X1, ident, ident16, ones, tri, rowmask, wsc, winv, gT, LG, W12H, W12L, W3H, W3L,
            xd, cd, zd, mask, gate_w, w12, w3):
    st = ExitStack()
    with st:
        def sb(name, shape, dt=F32):
            return st.enter_context(nc.sbuf_tensor(name, shape, dt))

        cs = sb("c_in", [P, Q, D])
        cT = sb("c_T", [P, 2, DC * P])
        y = sb("y", [P, Q, D])
        sm = sb("scores_T", [P, Q, P])
        z = sb("z", [P, Q, D])
        zp = sb("z_parts", [P, Q, 2 * D], F16)
        zT = sb("z_T", [P, 2, DC * P])
        stt = sb("moments_in", [P, 2 * Q, 6])
        mean, var, rst, tmp, nsc, nbi, unit = (sb(n, [P, 2 * Q]) for n in (
            "means", "vars", "rstds", "tmp8", "norm_scales", "norm_biases", "units"))
        wst = sb("w12_rows", [P, 2 * H // P, D])
        vst = sb("w3_rows", [P, DC, H])
        ss = sb("square_sums", [P, 1])
        tot = sb("total", [P, 1])
        ti = sb("exponent", [P, 1], I32)
        tj = sb("exponent_inv", [P, 1], I32)
        gs = zT[0:E, 0, :]
        ms = zp[0:T, 0, 0:P // 2].bitcast(U8)
        mf = zT[0:T, 1, 0:P]

        x_in, c_in, z_out = ([sem(f"{n}{k}") for k in range(Q)] for n in ("x_in", "c_in", "z_out"))
        g_in, m_in, w12_in, w3_in = sem("gate_in"), sem("mask_in"), [sem("w12_in0"), sem("w12_in1")], sem("w3_in")
        ones_made, made, unit_made, cast = (sem(n) for n in ("ones_made", "constants_made", "units_made", "mask_cast"))
        gate_turned, mask_turned, gate_kept = sem("gate_turned"), sem("mask_turned"), sem("gate_kept")
        x_stat, ct_made, ct_kept, y_made, xy_made = (sem(n) for n in (
            "x_stat", "ct_made", "ct_kept", "y_made", "xy_made"))
        sc_made, sm_made, qp_made, x1_made, x1_stat = (sem(n) for n in (
            "scores_made", "scores_masked", "qproj_made", "x1_made", "x1_stat"))
        z_made, zt_made, zt_kept, lg_made, lg_kept = (sem(n) for n in (
            "z_made", "zt_made", "zt_kept", "logits_made", "logits_kept"))
        zh_made, zl_made, norms_made = sem("z_high_made"), sem("z_low_made"), sem("norms_made")
        squared, totalled, scaled = sem("w12_squared"), sem("w12_totalled"), sem("w12_scaled")
        turned, high, low = sem("w_turned"), sem("w_high"), sem("w_low")
        NORM = NORM_N + 2
        SCALE = 8
        W = 6

        w12v = w12.rearrange("e (c p) d -> p e c d", p=P)
        w3v = w3.rearrange("e (c p) h -> p e c h", p=P)

        def at(i, k):
            return bass.ds(Q * i + k, 1)

        def x_row(i, k):
            return X1[:, at(i, k), :].rearrange("p a d -> p (a d)")

        def weights_at(i, g, w12x, w3x):
            e = bass.ds(i, 1)
            if g < 4:
                return w12x[:, e, g % 2, (g // 2) * H:(g // 2 + 1) * H].rearrange("p a h -> p (a h)")
            return w3x[:, e, 2 * (g - 4):2 * (g - 3), :].rearrange("p a c d -> p (a c d)")

        def schedule(eng, group):
            for i in range(3):
                group(i)
            with eng.Fori(3, NQ - 2) as i:
                group(i)
            for i in range(NQ - 2, NQ + 2):
                group(i)

        def inside(i):
            return not isinstance(i, int) or 0 <= i < NQ

        with nc.Block() as block:
            @block.sync
            def _(sp):
                def load_x(i, k):
                    after(sp, x_stat, Q * i + (k - 3))
                    sp.dma_start(X1[:, at(i, k), :], xd[:, at(i, k), :]).then_inc(x_in[k], 16)

                def load_c(i, k):
                    after(sp, ct_made, Q * i + (k - 3))
                    sp.dma_start(cs[:, k, :], cd[:, at(i, k), :]).then_inc(c_in[k], 16)

                def load_w12(i, half):
                    after(sp, turned, W * i + (2 * half - 4))
                    sp.dma_start(wst[:, 4 * half:4 * half + 4, :], w12v[:, bass.ds(i, 1), 4 * half:4 * half + 4, :])\
                        .then_inc(w12_in[half], 16)

                def load_w3(i):
                    after(sp, turned, W * i)
                    sp.dma_start(vst[:, :, :], w3v[:, bass.ds(i, 1), :, :]).then_inc(w3_in, 16)

                def store(i, k):
                    sp.wait_ge(zl_made, Q * i + (k + 1))
                    sp.dma_start(zd[:, at(i, k), :], zp[:, k, :]).then_inc(z_out[k], 16)

                sp.dma_start(gs, gate_w).then_inc(g_in, 16)
                sp.dma_start(ms, mask).then_inc(m_in, 16)
                for k in range(Q):
                    load_x(0, k)
                for k in range(Q):
                    load_c(0, k)
                load_w12(0, 0)
                load_w12(0, 1)
                load_w3(0)
                for k in range(Q):
                    load_x(1, k)

                def group(i):
                    if inside(i + 2):
                        for k in range(Q):
                            load_x(i + 2, k)
                    for k in range(Q):
                        if inside(i + 1):
                            load_c(i + 1, k)
                            if k % 2 == 1:
                                load_w12(i + 1, k // 2)
                    if inside(i - 2):
                        for k in range(Q):
                            store(i - 2, k)
                    if inside(i + 1):
                        load_w3(i + 1)

                schedule(sp, group)
                for k in range(Q):
                    sp.wait_ge(z_out[k], 16 * NQ)

            @block.gpsimd
            def _(pool):
                pool.memset(ones[:, :], 1.0).then_inc(ones_made, 1)
                pool.memset(ident[:, :], 0.0).then_inc(ones_made, 1)
                pool.wait_ge(ones_made, 2)
                pool.affine_select(out=ident[:, :], in_=ident[:, :], compare_op=ALU.not_equal, fill=1.0,
                                   base=0, pattern=[[-1, P]], channel_multiplier=1).then_inc(made, 1)
                pool.affine_select(out=tri[:, :], in_=ones[:, :], compare_op=ALU.is_ge, fill=0.0,
                                   base=0, pattern=[[1, P]], channel_multiplier=-1).then_inc(made, 1)
                pool.wait_ge(made, 2)
                pool.tensor_copy(ident16[:, :], ident[:, :]).then_inc(made, 1)

                def add_y(i, k):
                    apart(pool, y_made, Q * i + (k + 1))
                    pool.tensor_tensor(x_row(i, k), x_row(i, k), y[:, k, :], ALU.add).then_inc(xy_made, 1)

                def part_z(i, k):
                    after(pool, z_out[k], 16 * i)
                    apart(pool, z_made, Q * i + (k + 1))
                    pool.tensor_copy(zp[:, k, 0:D], z[:, k, :]).then_inc(zh_made, 1)
                    pool.wait_ge(zh_made, Q * i + (k + 1))
                    pool.tensor_tensor(zp[:, k, D:2 * D], z[:, k, :], zp[:, k, 0:D], ALU.subtract)\
                        .then_inc(zl_made, 1)

                pool.wait_ge(cast, 1)

                def group(i):
                    for k in range(Q):
                        if inside(i):
                            add_y(i, k)
                        if inside(i - 2):
                            part_z(i - 2, k)

                schedule(pool, group)

            @block.scalar
            def _(act):
                a = nc.scalar

                def square(i):
                    act.wait_ge(w12_in[0], 16 * i + 16)
                    act.wait_ge(w12_in[1], 16 * i + 16)
                    after(act, totalled, i)
                    act.nop(nofuse=True)
                    a.activation(W12L[:, bass.ds(i, 1), :, :].rearrange("p a c (b d) -> p (a c b) d", d=D).bitcast(BF16),
                                 wst[:, :, :], ACT.Square, accum_out=ss[:, 0:1]).then_inc(squared, 1)

                def make_y(i, k):
                    after(act, qp_made, Q * i + (k - 3))
                    act.wait_ge(x_in[k], 16 * i + 16)
                    apart(act, norms_made, NORM * i + NORM)
                    a.activation(y[:, k, :], x_row(i, k), ACT.Identity, scale=nsc[:, Q + k:Q + k + 1],
                                 bias=nbi[:, Q + k:Q + k + 1]).then_inc(y_made, 1)

                def keep_ct(i, k):
                    after(act, sc_made, Q * i + (k - 1))
                    act.wait_ge(ct_made, Q * i + (k + 1))
                    a.activation(cT[:, k % 2, :], PS[:, 0, 0:D], ACT.Copy).then_inc(ct_kept, 1)

                def make_z(i, k):
                    after(act, zl_made, Q * i + (k - 3))
                    after(act, zt_made, Q * i + (k - 3))
                    apart(act, norms_made, NORM * (i + 3))
                    a.activation(z[:, k, :], x_row(i, k), ACT.Identity, scale=nsc[:, k:k + 1],
                                 bias=nbi[:, k:k + 1]).then_inc(z_made, 1)

                def keep_zt(i, k):
                    after(act, lg_made, Q * i + (k - 1))
                    act.wait_ge(zt_made, Q * i + (k + 1))
                    a.activation(zT[:, k % 2, :], PS[:, 4, 0:D], ACT.Copy).then_inc(zt_kept, 1)

                def part_w(i, g):
                    if g == 0:
                        act.wait_ge(scaled, SCALE * i + SCALE)
                    apart(act, turned, W * i + (g + 1))
                    src = PS[:, 6 + g % 2, :]
                    dst = weights_at(i, g, W12H, W3H)
                    if g < 4:
                        a.activation(dst, src, ACT.Copy, scale=wsc[:, bass.ds(i, 1)]).then_inc(high, 1)
                    else:
                        a.activation(dst, src, ACT.Copy).then_inc(high, 1)

                act.wait_ge(gate_kept, 2)

                def group(i):
                    for k in range(W + 1):
                        if k < Q and inside(i):
                            keep_ct(i, k)
                            make_y(i, k)
                        if k < Q and inside(i - 2):
                            make_z(i - 2, k)
                        if k >= 1 and inside(i):
                            part_w(i, k - 1)
                        if 1 <= k <= Q and inside(i - 2):
                            keep_zt(i - 2, k - 1)
                    if inside(i + 1):
                        square(i + 1)

                square(0)
                schedule(act, group)

            @block.tensor
            def _(pe):
                def turn_c(i, k):
                    after(pe, ct_kept, Q * i + k)
                    pe.wait_ge(c_in[k], 16 * i + 16)
                    for c in range(DC):
                        mm = pe.transpose(PS[:, 0, c * P:(c + 1) * P], cs[:, k, c * P:(c + 1) * P], ident[:, :])
                    mm.then_inc(ct_made, 1)

                def turn_w(i, g):
                    after(pe, low, W * i + (g - 1))
                    if g in (0, 2):
                        pe.wait_ge(w12_in[g // 2], 16 * i + 16)
                    if g == 4:
                        pe.wait_ge(w3_in, 16 * i + 16)
                    for n in range(4):
                        if g < 4:
                            c, b = g % 2, 4 * (g // 2) + n
                            src = wst[:, b, c * P:(c + 1) * P]
                        else:
                            c, b = n % 2, 2 * (g - 4) + n // 2
                            src = vst[:, c, b * P:(b + 1) * P]
                        mm = pe.transpose(PS[:, 6 + g % 2, n * P:(n + 1) * P], src, ident[:, :])
                    mm.then_inc(turned, 1)

                def scores(i, k):
                    after(pe, sm_made, Q * i + k)
                    pe.wait_ge(ct_kept, Q * i + (k + 1))
                    for c in range(DC):
                        chunk = cT[:, k % 2, c * P:(c + 1) * P]
                        mm = pe.matmul(PS[:, 1, 0:P], chunk, chunk, start=(c == 0), stop=(c == DC - 1))
                    mm.then_inc(sc_made, 1)

                def product(i, k):
                    after(pe, x1_made, Q * i + (k - 1))
                    pe.wait_ge(sm_made, Q * i + (k + 1))
                    pe.wait_ge(y_made, Q * i + (k + 1))
                    pe.matmul(PS[:, 2 + k % 2, 0:D], sm[:, k, :], y[:, k, :], start=True, stop=True)\
                        .then_inc(qp_made, 1)

                def turn_z(i, k):
                    after(pe, zt_kept, Q * i + k)
                    pe.wait_ge(z_made, Q * i + (k + 1))
                    for c in range(DC):
                        mm = pe.transpose(PS[:, 4, c * P:(c + 1) * P], z[:, k, c * P:(c + 1) * P], ident[:, :])
                    mm.then_inc(zt_made, 1)

                def logits(i, k):
                    if k == 0:
                        after(pe, lg_kept, i)
                        pe.wait_ge(scaled, SCALE * NQ if isinstance(i, int) and i + 3 > NQ else SCALE * (i + 2) + 1)
                    pe.wait_ge(zt_kept, Q * i + (k + 1))
                    for c in range(DC):
                        mm = pe.matmul(PS[:, 5, k * E:(k + 1) * E], zT[:, k % 2, c * P:(c + 1) * P], gT[:, c, :],
                                       start=(c == 0), stop=(c == DC - 1))
                    mm.then_inc(lg_made, 1)

                def total(i):
                    after(pe, scaled, SCALE * i)
                    after(pe, lg_kept, i - 2)
                    pe.wait_ge(squared, i + 1)
                    pe.matmul(PS[:, 5, Q * E:Q * E + 1], ones[:, :], ss[:, :], start=True, stop=True)\
                        .then_inc(totalled, 1)

                pe.wait_ge(made, 3)
                pe.wait_ge(g_in, 16)
                for c in range(DC):
                    mm = pe.transpose(PS[:, 4, c * E:(c + 1) * E], gs[:, c * P:(c + 1) * P], ident[0:E, 0:E])
                mm.then_inc(gate_turned, 1)
                pe.wait_ge(cast, 1)
                pe.transpose(PS[:, 5, 0:T], mf, ident[0:T, 0:T]).then_inc(mask_turned, 1)
                pe.wait_ge(gate_kept, 2)

                def group(i):
                    for k in range(W + 1):
                        if k == 0 and inside(i):
                            turn_c(i, 0)
                            total(i)
                        if k >= 1 and inside(i):
                            turn_w(i, k - 1)
                        if 1 <= k <= Q:
                            if inside(i):
                                scores(i, k - 1)
                            if inside(i - 2):
                                turn_z(i - 2, k - 1)
                        if k + 1 < Q and inside(i):
                            turn_c(i, k + 1)
                        if 2 <= k <= Q + 1:
                            if inside(i):
                                product(i, k - 2)
                            if inside(i - 2):
                                logits(i - 2, k - 2)

                schedule(pe, group)

            @block.vector
            def _(dve):
                v = nc.vector

                def x_moments(i, k):
                    apart(dve, x_in[k], 16 * i + 16)
                    v.bn_stats(stt[:, Q + k, :], x_row(i, k)).then_inc(x_stat, 1)

                def mask_scores(i, k):
                    after(dve, qp_made, Q * i + (k - 3))
                    dve.wait_ge(sc_made, Q * i + (k + 1))
                    v.tensor_tensor(sm[:, k, :], PS[:, 1, 0:P], tri[:, :], ALU.mult).then_inc(sm_made, 1)

                def add_product(i, k):
                    dve.wait_ge(qp_made, Q * i + (k + 1))
                    dve.wait_ge(xy_made, Q * i + (k + 1))
                    v.tensor_tensor(x_row(i, k), PS[:, 2 + k % 2, 0:D], x_row(i, k), ALU.add).then_inc(x1_made, 1)

                def x1_moments(i, k):
                    apart(dve, x1_made, Q * i + (k + 1))
                    v.bn_stats(stt[:, k, :], x_row(i, k)).then_inc(x1_stat, 1)

                def norms(i):
                    lo, hi = (0 if inside(i - 1) else Q), (2 * Q if inside(i + 1) else Q)
                    if inside(i - 1):
                        dve.wait_ge(x1_stat, Q * i)
                    if inside(i + 1):
                        dve.wait_ge(x_stat, Q * i + 2 * Q)
                    after(dve, norms_made, NORM * (i + 1))
                    ch = Chain(dve, norms_made, NORM * (i + 1))
                    m, vr, r, u = (t[:, lo:hi] for t in (mean, var, rst, tmp))
                    yield from moments(v, ch, stt[:, lo:hi, :], m, vr, u)
                    ch.join()
                    ch.post(v.tensor_scalar(vr, vr, LN_EPS, None, ALU.add))
                    yield
                    yield from rsqrt_steps(v, ch, r, vr, u)
                    ch.join()
                    after(dve, y_made, min(Q * i + Q, T) if isinstance(i, int) else Q * i + Q)
                    after(dve, z_made, Q * (i - 1))
                    ch.post(v.tensor_tensor(nsc[:, lo:hi], r, unit[:, lo:hi], ALU.mult))
                    yield
                    ch.join()
                    ch.post(v.scalar_tensor_tensor(out=nbi[:, lo:hi], in0=m, scalar=-1.0, in1=nsc[:, lo:hi],
                                                   op0=ALU.mult, op1=ALU.mult))
                    assert ch.n == NORM

                def keep_logits(i):
                    dve.wait_ge(lg_made, Q * i + Q)
                    v.tensor_copy(LG[:, i * Q:(i + 1) * Q, :] if isinstance(i, int) else LG[:, bass.ds(i * Q, Q), :],
                                  PS[:, 5, 0:Q * E].rearrange("p (t e) -> p t e", t=Q)).then_inc(lg_kept, 1)

                def scale(i):
                    ch = Chain(dve, scaled, SCALE * i)
                    dve.wait_ge(totalled, i + 1)
                    ch.post(v.tensor_copy(tot[:, :], PS[:, 5, Q * E:Q * E + 1]))
                    yield
                    ch.join()
                    ch.post(v.tensor_scalar(ti[:, :], tot[:, :].bitcast(I32), 23, None, ALU.logical_shift_right))
                    yield
                    ch.join()
                    ch.post(v.tensor_scalar(ti[:, :], ti[:, :], 1, None, ALU.add))
                    yield
                    ch.join()
                    ch.post(v.tensor_scalar(ti[:, :], ti[:, :], 1, None, ALU.logical_shift_right))
                    yield
                    ch.join()
                    ch.post(v.tensor_scalar(tj[:, :], ti[:, :], 39, None, ALU.add))
                    ch.post(v.tensor_scalar(ti[:, :], ti[:, :], -1, 205, ALU.mult, ALU.add))
                    yield
                    ch.join()
                    dve.nop(nofuse=True)
                    ch.post(v.tensor_scalar(wsc[:, bass.ds(i, 1)].bitcast(I32), ti[:, :], 23, None,
                                            ALU.logical_shift_left))
                    ch.post(v.tensor_scalar(winv[:, bass.ds(i, 1)].bitcast(I32), tj[:, :], 23, None,
                                            ALU.logical_shift_left))
                    ch.join()
                    assert ch.n == SCALE

                def part_w(i, g):
                    dve.wait_ge(high, W * i + (g + 1))
                    src = PS[:, 6 + g % 2, :]
                    if g < 4:
                        v.scalar_tensor_tensor(out=weights_at(i, g, W12L, W3L), in0=src, scalar=wsc[:, bass.ds(i, 1)],
                                               in1=weights_at(i, g, W12H, W3H), op0=ALU.mult, op1=ALU.subtract)\
                            .then_inc(low, 1)
                    else:
                        v.tensor_tensor(weights_at(i, g, W12L, W3L), src, weights_at(i, g, W12H, W3H).bitcast(F32),
                                        ALU.subtract).then_inc(low, 1)

                v.memset(unit[:, 0:Q], Z_SCALE).then_inc(unit_made, 1)
                v.memset(unit[:, Q:2 * Q], 1.0).then_inc(unit_made, 1)
                dve.wait_ge(m_in, 16)
                v.tensor_copy(mf, ms).then_inc(cast, 1)
                dve.wait_ge(gate_turned, 1)
                v.tensor_scalar(gT[:, :, :], PS[:, 4, 0:DC * E].rearrange("p (c e) -> p c e", c=DC),
                                1.0 / Z_SCALE, None, ALU.mult).then_inc(gate_kept, 1)
                dve.wait_ge(mask_turned, 1)
                v.tensor_scalar(rowmask[:, :], PS[:, 5, 0:T], -NEG_BIG, NEG_BIG, ALU.mult, ALU.add).then_inc(gate_kept, 1)
                for k in range(Q):
                    x_moments(0, k)
                dve.wait_ge(unit_made, 2)
                advance(norms(-1), NORM)

                def group(i):
                    norm_links = norms(i) if inside(i - 1) or inside(i + 1) else iter(())
                    scale_links = scale(i) if inside(i) else iter(())
                    for k in range(6):
                        advance(scale_links, 1)
                        advance(norm_links, 1 if k >= Q else 0)
                    for k in range(W + 1):
                        advance(norm_links, 1)
                        if k >= 1 and inside(i):
                            part_w(i, k - 1)
                        if k >= 1:
                            advance(norm_links, 1)
                        if 1 <= k <= Q and inside(i):
                            mask_scores(i, k - 1)
                        if 2 <= k <= Q + 1 and inside(i):
                            add_product(i, k - 2)
                        if 3 <= k <= Q + 2 and inside(i):
                            x1_moments(i, k - 3)
                        if k == W and inside(i - 2):
                            keep_logits(i - 2)
                    advance(norm_links, NORM)
                    if inside(i + 2):
                        for k in range(Q):
                            x_moments(i + 2, k)

                for k in range(Q):
                    x_moments(1, k)
                schedule(dve, group)
                dve.wait_ge(lg_kept, NQ)


def route(nc, sem, PS, ones, ident16, LG, winv, prob, ye_idx, tok_idx, blk_exp, blk_inv, wmean, magic, w1q, w2q,
          w1, w2):
    st = ExitStack()
    with st:
        def sb(name, shape, dt=F32):
            return st.enter_context(nc.sbuf_tensor(name, shape, dt))

        rev_e = sb("rev_expert", [P, E])
        col = sb("column", [P, P])
        tok = sb("token_id", [P, T, 2])
        lower = sb("lower", [P, P])
        edge_t = sb("edges", [P, T])
        exp_e = sb("expert_id", [P, E])
        blk_j = sb("block_id", [P, NBE])
        first = sb("first", [P, T, E])
        second = sb("second", [P, T, E])
        both = sb("both", [P, T, E])
        a1 = sb("work1", [P, T, E])
        a2 = sb("work2", [P, T, E])
        m1, m2, c1, dl, e2, r2 = (sb(n, [P, T]) for n in ("max1", "max2", "code", "gap", "exp_gap", "rsum"))
        tile_n = a2[:, :, :].rearrange("p t e -> p (t e)").rearrange("p (e t) -> p e t", e=E)
        incl = sb("inclusive", [P, E, T])
        excl = sb("exclusive", [P, E, T])
        tot, nblk, bend, base = (sb(n, [P, E]) for n in ("totals8", "blocks8", "block_end", "base8"))
        pos = sb("places", [P, T, 2])
        posi = sb("places_int", [P, 2 * T], I32)
        low = sb("place_low", [P, 2 * T])
        high = sb("place_high", [P, 2 * T])
        b1_ = sb("block_work", [P, NBE, E])
        be = sb("block_expert_f", [P, NBE])
        lo_hot = sb("low_hot", [P, 2, Q, P], F32R)
        hi_hot = sb("high_hot", [P, 2, Q, NBE], F32R)

        wst = sb("w12_ffn_rows", [P, 2, 2 * F])
        wt = (w2q[:, :, :].rearrange("p c d -> p (c d)").bitcast(F16), wst[:, 0, 0:F].bitcast(F16))
        rev = rev_e[:, :].unsqueeze(1).broadcast_to([P, T, E])
        edge = edge_t[:, :].unsqueeze(1).broadcast_to([P, E, T])
        one8 = ones[:, 0:1].broadcast_to([P, E * T])
        sums = sb("abs_sums", [P, 2])
        rec = sb("w_scales", [P, 2])

        made = sem("route_constants")
        w_in = [sem("w1_in"), sem("w2_in")]
        w_summed, w_total, mean_made = (sem("w_" + n) for n in ("summed", "totalled", "mean"))
        rec_made, magic_made, w_round, w_sign, w_turned, w_kept = (sem("w_" + n) for n in (
            "scale", "magic", "rounded", "ternary", "turned_ffn", "kept"))
        dch = sem("route_dve")
        gap, exped = sem("gap_ready"), sem("gap_exped")
        counted = sem("counted")
        hot, named, placed = sem("hot_made"), sem("hot_named"), sem("placed")
        BATCHES = 2 * T // Q

        def rows(n, t):
            return t.rearrange("p (c w) -> p c w", w=(D, F)[n])

        with nc.Block() as block:
            @block.sync
            def _(sp):
                for n, w in enumerate((w1, w2)):
                    sp.dma_start(rows(n, wst[:, n, :]), w.rearrange("(c p) w -> p c w", p=P)).then_inc(w_in[n], 16)

            @block.gpsimd
            def _(pool):
                pool.memset(magic[:, 0:1], ROUND).then_inc(magic_made, 1)
                pool.memset(magic[:, 1:2], -ROUND).then_inc(magic_made, 1)

                def iota(ap, pattern, base, mult):
                    pool.iota(ap, pattern, base=base, channel_multiplier=mult,
                              allow_small_or_imprecise_dtypes=True).then_inc(made, 1)

                iota(rev_e[:, :], [[-1, E]], E, 0)
                iota(col[:, :], [[1, P]], 0, 0)
                iota(tok[:, :, :], [[P, T], [0, 2]], 0, 1)
                iota(edge_t[:, :], [[P, T]], 0, 0)
                iota(exp_e[:, :], [[1, E]], 0, 0)
                iota(blk_j[:, :], [[1, NBE]], 0, 0)
                pool.affine_select(out=lower[:, :], in_=ones[:, :], compare_op=ALU.is_gt, fill=0.0,
                                   base=0, pattern=[[1, P]], channel_multiplier=-1).then_inc(made, 1)

                def name_tokens(b, slot):
                    apart(pool, hot, 2 * b + 2)
                    ids = tok[:, :, :].rearrange("p t k -> p (t k)")[:, bass.ds(Q * b, Q)]
                    pool.tensor_tensor(hi_hot[:, slot, :, :], hi_hot[:, slot, :, :].bitcast(F32),
                                       ids.unsqueeze(2).broadcast_to([P, Q, NBE]), ALU.mult).then_inc(named, 1)

                with pool.Fori(0, BATCHES // 2) as i:
                    for slot in range(2):
                        name_tokens(2 * i + slot, slot)

            @block.scalar
            def _(act):
                act.wait_ge(magic_made, 2)
                for n in range(2):
                    act.wait_ge(w_in[n], 16)
                    after(act, w_summed, n)
                    act.activation(wt[0], wst[:, n, :], ACT.Abs, accum_out=sums[:, n:n + 1]).then_inc(w_summed, 1)
                act.wait_ge(gap, 1)
                act.activation(e2[:, :], dl[:, :], ACT.Exp).then_inc(exped, 1)
                act.wait_ge(w_summed, 2)
                for n in range(2):
                    act.wait_ge(rec_made, n + 1)
                    act.activation(wst[:, n, :], wst[:, n, :], ACT.Identity, scale=rec[:, n:n + 1], bias=magic[:, 0:1])\
                        .then_inc(w_round, 1)
                    act.wait_ge(w_round, n + 1)
                    act.activation(wt[n], wst[:, n, :], ACT.Sign, bias=magic[:, 1:2]).then_inc(w_sign, 1)
                    for m in range(2):
                        act.wait_ge(w_turned, 2 * n + m + 1)
                        src = PS[:, 3 + m, :].bitcast(F16)
                        if n == 0:
                            act.activation(w1q[:, m, :], src, ACT.Copy).then_inc(w_kept, 1)
                        else:
                            act.activation(w2q[:, 4 * m:4 * m + 4, :], src.rearrange("p (c d) -> p c d", d=D),
                                           ACT.Copy).then_inc(w_kept, 1)

            @block.tensor
            def _(pe):
                def total(n):
                    pe.wait_ge(w_summed, n + 1)
                    pe.matmul(PS[:, 5 + n, 0:1], ones[:, :], sums[:, n:n + 1], start=True, stop=True)\
                        .then_inc(w_total, 1)

                def turn_w(n):
                    pe.wait_ge(w_sign, n + 1)
                    after(pe, w_kept, 2 * n)
                    for m in range(2):
                        for c in range(8):
                            if n == 0:
                                src = rows(0, wt[0])[:, c, m * P:(m + 1) * P]
                            else:
                                hc, d = 4 * m + c // 2, c % 2
                                src = rows(1, wt[1])[:, d, hc * P:(hc + 1) * P]
                            mm = pe.transpose(PS[:, 3 + m, :].bitcast(F16)[:, c * P:(c + 1) * P], src, ident16[:, :])
                        mm.then_inc(w_turned, 1)

                pe.wait_ge(made, 7)
                pe.wait_ge(dch, ROUTE_BOTH)
                flat = both[:, :, :].rearrange("p t e -> p (t e)")
                pe.matmul(PS[:, 0, 0:T * E], lower[:, :], flat, start=True, stop=True).then_inc(counted, 1)
                pe.matmul(PS[:, 1, 0:T * E], ones[:, :], flat, start=True, stop=True).then_inc(counted, 1)

                total(0)
                total(1)

                def place(b, slot, start=False, stop=False):
                    pe.wait_ge(named, b + 1)
                    for u in range(Q):
                        mm = pe.matmul(PS[:, 2, 0:NBE], lo_hot[:, slot, u, :], hi_hot[:, slot, u, :],
                                       start=start and u == 0, stop=stop and u == Q - 1, skip_group_check=True)
                    mm.then_inc(placed, 1)

                place(0, 0, start=True)
                place(1, 1)
                turn_w(0)
                with pe.Fori(1, BATCHES // 2 - 1) as i:
                    for slot in range(2):
                        place(2 * i + slot, slot)
                place(BATCHES - 2, 0)
                place(BATCHES - 1, 1, stop=True)
                turn_w(1)

            @block.vector
            def _(dve):
                ch = Chain(dve, dch, 0)
                v = nc.vector

                def over_e(a):
                    return a.unsqueeze(2).broadcast_to([P, T, E])

                def over_t(a):
                    return a.unsqueeze(2).broadcast_to([P, E, T])

                def pick(logits, top, code, one_hot):
                    ch.link(v.tensor_reduce(top[:, :], logits[:, :, :], AX_X, ALU.max))
                    ch.link(v.tensor_tensor(a1[:, :, :], logits[:, :, :], over_e(top[:, :]), ALU.is_equal))
                    ch.link(v.tensor_tensor(a1[:, :, :], a1[:, :, :], rev, ALU.mult))
                    ch.link(v.tensor_reduce(code[:, :], a1[:, :, :], AX_X, ALU.max))
                    ch.link(v.tensor_tensor(one_hot[:, :, :], rev, over_e(code[:, :]), ALU.is_equal))

                dve.wait_ge(made, 7)
                pick(LG, m1, c1, first)
                ch.link(v.scalar_tensor_tensor(out=a2[:, :, :], in0=first[:, :, :], scalar=-HUGE, in1=LG[:, :, :],
                                               op0=ALU.mult, op1=ALU.add))
                pick(a2, m2, c1, second)
                ch.link(v.tensor_tensor(both[:, :, :], first[:, :, :], second[:, :, :], ALU.add))
                assert ch.n == ROUTE_BOTH

                def mean_of(n):
                    dve.wait_ge(w_total, n + 1)
                    v.tensor_scalar(wmean[:, n:n + 1], PS[:, 5 + n, 0:1], 1.0 / (D * F), QUANT_EPS, ALU.mult, ALU.max)\
                        .then_inc(mean_made, 1)
                    dve.wait_ge(mean_made, n + 1)
                    v.reciprocal(rec[:, n:n + 1], wmean[:, n:n + 1]).then_inc(rec_made, 1)

                v.tensor_tensor(dl[:, :], m2[:, :], m1[:, :], ALU.subtract).then_inc(gap, 1)
                for n in range(2):
                    mean_of(n)
                dve.wait_ge(counted, 2)
                ch.link(v.tensor_copy(tile_n, PS[:, 1, 0:T * E].rearrange("p (t e) -> p e t", e=E)))
                flat_n, flat_i, flat_x = (a.rearrange("p e t -> p (e t)") for a in (tile_n, incl[:, :, :], excl[:, :, :]))
                ch.link(v.tensor_tensor_scan(flat_i, one8, flat_n, 0.0, ALU.mult, ALU.add))
                ch.link(v.tensor_tensor(flat_x, flat_i, flat_n, ALU.subtract))
                ch.link(v.tensor_tensor(tot[:, :], incl[:, :, T - 1], excl[:, :, 0], ALU.subtract))
                ch.link(v.tensor_tensor(incl[:, :, :], over_t(tot[:, :]), edge, ALU.is_gt))
                ch.link(v.tensor_reduce(nblk[:, :], incl[:, :, :], AX_X, ALU.add))
                ch.link(v.tensor_tensor_scan(bend[:, :], ones[:, 0:E], nblk[:, :], 0.0, ALU.mult, ALU.add))
                ch.link(v.tensor_tensor(base[:, :], bend[:, :], nblk[:, :], ALU.subtract))
                ch.link(v.scalar_tensor_tensor(out=base[:, :], in0=base[:, :], scalar=float(P), in1=excl[:, :, 0],
                                               op0=ALU.mult, op1=ALU.subtract))
                ch.link(v.tensor_tensor(incl[:, :, :], excl[:, :, :], over_t(base[:, :]), ALU.add))
                ch.link(v.tensor_tensor(a1[:, :, :], PS[:, 0, 0:T * E].rearrange("p (t e) -> p t e", e=E),
                                        incl[:, :, :].rearrange("p e t -> p t e"), ALU.add))
                for k, hot_k in enumerate((first, second)):
                    ch.link(v.tensor_tensor(a2[:, :, :], hot_k[:, :, :], a1[:, :, :], ALU.mult))
                    ch.link(v.tensor_reduce(pos[:, :, k], a2[:, :, :], AX_X, ALU.add))
                flat_pos = pos[:, :, :].rearrange("p t k -> p (t k)")
                ch.post(v.tensor_copy(ye_idx[:, :, :], pos[:, :, :]))
                ch.link(v.tensor_copy(posi[:, :], flat_pos))
                ch.link(v.tensor_scalar(low[:, :].bitcast(I32), posi[:, :], P - 1, None, ALU.bitwise_and))
                ch.link(v.tensor_copy(low[:, :], low[:, :].bitcast(I32)))
                ch.link(v.tensor_scalar(high[:, :].bitcast(I32), posi[:, :], 7, None, ALU.logical_shift_right))
                ch.link(v.tensor_copy(high[:, :], high[:, :].bitcast(I32)))

                def heat(b, slot):
                    after(dve, placed, b - 1)
                    at = bass.ds(Q * b, Q)
                    v.tensor_tensor(lo_hot[:, slot, :, :], col[:, :].unsqueeze(1).broadcast_to([P, Q, P]),
                                    low[:, at].unsqueeze(2).broadcast_to([P, Q, P]), ALU.is_equal).then_inc(hot, 1)
                    v.tensor_tensor(hi_hot[:, slot, :, :], blk_j[:, :].unsqueeze(1).broadcast_to([P, Q, NBE]),
                                    high[:, at].unsqueeze(2).broadcast_to([P, Q, NBE]), ALU.is_equal).then_inc(hot, 1)

                assert ch.n == ROUTE_PLACES
                heat(0, 0)
                heat(1, 1)
                with dve.Fori(1, BATCHES // 2) as i:
                    for slot in range(2):
                        heat(2 * i + slot, slot)
                ch.link(v.tensor_tensor(b1_[:, :, :], blk_j[:, :].unsqueeze(2).broadcast_to([P, NBE, E]),
                                        bend[:, :].unsqueeze(1).broadcast_to([P, NBE, E]), ALU.is_ge))
                ch.link(v.tensor_reduce(be[:, :], b1_[:, :, :], AX_X, ALU.add))
                ch.link(v.tensor_scalar(be[:, :], be[:, :], float(E - 1), None, ALU.min))
                ch.post(v.tensor_copy(blk_exp[:, :], be[:, :]))
                ch.link(v.tensor_tensor(b1_[:, :, :], exp_e[:, :].unsqueeze(1).broadcast_to([P, NBE, E]),
                                        be[:, :].unsqueeze(2).broadcast_to([P, NBE, E]), ALU.is_equal))
                ch.link(v.tensor_tensor(b1_[:, :, :], b1_[:, :, :],
                                        winv[:, :].unsqueeze(1).broadcast_to([P, NBE, E]), ALU.mult))
                ch.link(v.tensor_reduce(blk_inv[:, :], b1_[:, :, :], AX_X, ALU.add))
                dve.wait_ge(exped, 1)
                ch.link(v.tensor_scalar(r2[:, :], e2[:, :], 1.0, None, ALU.add))
                ch.link(v.reciprocal(prob[:, 0, :], r2[:, :]))
                ch.link(v.tensor_tensor(prob[:, 1, :], e2[:, :], prob[:, 0, :], ALU.mult))
                dve.wait_ge(placed, BATCHES)
                ch.link(v.tensor_copy(tok_idx[:, :], PS[:, 2, 0:NBE]))


ROUTE_BOTH = 12
ROUTE_PLACES = ROUTE_BOTH + 21


def experts(nc, sem, PS, ident, ident16, W12H, W12L, W3H, W3L, blk_inv, blk_exp, tok_idx, z_dram, yd):
    st = ExitStack()
    with st:
        def sb(name, shape, dt=F32):
            return st.enter_context(nc.sbuf_tensor(name, shape, dt))

        idx = sb("block_tokens", [P, 2], U32)
        zg = sb("z_gathered", [P, 2, 2 * D], F16)
        zT = sb("z_turned", [P, 2, 2 * D], F16)
        s = sb("silu", [P, 2, H])
        g = sb("hidden", [P, 2, H])
        gh = sb("hidden_T_high", [P, 2, H], F32R)
        gl = sb("hidden_T_low", [P, 2, H], F32R)
        ye = sb("expert_out", [P, 2, D])

        z_in = [sem("z_gathered0"), sem("z_gathered1")]
        ye_out = [sem("ye_out0"), sem("ye_out1")]
        idx_made = sem("idx_made")
        zt_made, zt_kept, h1_made, h2_made, s_made, g_made = (sem("moe_" + n) for n in (
            "zt", "zt_kept", "h1", "h2", "silu", "hidden"))
        gt_made, gh_made, gl_made, y_made, ye_made = (sem("moe_" + n) for n in (
            "hidden_turned", "hidden_high", "hidden_low", "y", "ye"))
        PAIRS = (NB - 3) // 2
        REST = range(2 * PAIRS, NB)

        def steps(eng, first, step):
            first()
            for j in range(2):
                step(j, j, True, True)
            with eng.Fori(1, PAIRS) as i:
                for u in range(2):
                    step(2 * i + u, u, True, True)
            for j in REST:
                step(j, j % 2, j + 1 < NB, j + 2 < NB)
            step(NB, NB % 2, False, False)

        with nc.Block() as block:
            @block.gpsimd
            def _(pool):
                def gather(j, u, i2):
                    after(pool, z_in[u], 8 * i2)
                    pool.tensor_copy(idx[:, u:u + 1], tok_idx[:, bass.ds(j, 1)]).then_inc(idx_made, 1)
                    after(pool, zt_made, i2)
                    apart(pool, idx_made, j + 1)
                    pool.indirect_dma_start(zg[:, u, :], None, z_dram[:, :],
                                            bass.IndirectOffsetOnAxis(ap=idx[:, u:u + 1], axis=0)).then_inc(z_in[u], 16)

                for j in range(2):
                    gather(j, j, 0)
                with pool.Fori(1, NB // 2) as i:
                    for u in range(2):
                        gather(2 * i + u, u, 2 * i)
                gather(NB - 1, 0, NB - 1)

            @block.sync
            def _(sp):
                def store(j, u):
                    sp.wait_ge(ye_made, j + 1)
                    sp.dma_start(yd[:, bass.ds(j, 1), :], ye[:, u, :]).then_inc(ye_out[u], 16)

                with sp.Fori(0, NB // 2) as i:
                    for u in range(2):
                        store(2 * i + u, u)
                store(NB - 1, 0)
                sp.wait_ge(ye_out[0], 16 * (NB // 2 + 1))
                sp.wait_ge(ye_out[1], 16 * (NB // 2))

            @block.tensor
            def _(pe):
                def turn_z(j, u):
                    after(pe, zt_kept, j)
                    pe.wait_ge(z_in[u], 8 * (j - u) + 16)
                    for c in range(2 * DC):
                        mm = pe.transpose(PS[:, 0, 0:D].bitcast(F16)[:, c * P:(c + 1) * P],
                                          zg[:, u, c * P:(c + 1) * P], ident16[:, :])
                    mm.then_inc(zt_made, 1)

                def expert(j):
                    return bass.ds(pe.value_load(blk_exp[0:1, bass.ds(j, 1)], min_val=0, max_val=E - 1), 1)

                def up(j, u, e):
                    pe.wait_ge(zt_kept, j + 1)
                    for half, freed, made in ((0, s_made, h1_made), (1, g_made, h2_made)):
                        after(pe, freed, j - 1)
                        n = 0
                        for c in range(DC):
                            for part, w in ((0, W12L), (0, W12H), (1, W12H)):
                                k = part * DC + c
                                mm = pe.matmul(PS[:, 1 + half + 2 * u, :], zT[:, u, k * P:(k + 1) * P],
                                               w[:, e, c, half * H:(half + 1) * H].rearrange("p a h -> p (a h)"),
                                               start=(n == 0), stop=(n == 3 * DC - 1))
                                n += 1
                        mm.then_inc(made, 1)

                def turn_g(j, u):
                    after(pe, gl_made, j)
                    pe.wait_ge(g_made, j + 1)
                    for c in range(HC):
                        mm = pe.transpose(PS[:, 5, c * P:(c + 1) * P], g[:, u, c * P:(c + 1) * P], ident[:, :])
                    mm.then_inc(gt_made, 1)

                def down(j, u, e):
                    pe.wait_ge(gl_made, j + 1)
                    after(pe, ye_made, j - 1)
                    n = 0
                    for c in range(HC):
                        for gg, w in ((gh, W3L), (gh, W3H), (gl, W3H)):
                            mm = pe.matmul(PS[:, 6 + u, 0:D], gg[:, u, c * P:(c + 1) * P],
                                           w[:, e, c, :].rearrange("p a d -> p (a d)"),
                                           start=(n == 0), stop=(n == 3 * HC - 1))
                            n += 1
                    mm.then_inc(y_made, 1)

                def first():
                    for j in range(2):
                        turn_z(j, j)
                        up(j, j, expert(j))

                def step(j, u, more, more2):
                    before = not (isinstance(j, int) and j == 0)
                    if before:
                        e_down = expert(j - 1)
                    if more2:
                        e_up = expert(j + 2)
                    if not (isinstance(j, int) and j == NB):
                        turn_g(j, u)
                    if more2:
                        turn_z(j + 2, u)
                    if before:
                        down(j - 1, 1 - u, e_down)
                    if more2:
                        up(j + 2, u, e_up)

                steps(pe, first, step)

            @block.scalar
            def _(act):
                a = nc.scalar

                def keep_zt(j, u):
                    after(act, h2_made, j - 1)
                    act.wait_ge(zt_made, j + 1)
                    a.activation(zT[:, u, :], PS[:, 0, 0:D].bitcast(F16), ACT.Copy).then_inc(zt_kept, 1)

                def silu(j, u):
                    apart(act, h1_made, j + 1)
                    after(act, g_made, j - 1)
                    act.nop(nofuse=True)
                    a.activation(s[:, u, :], PS[:, 1 + 2 * u, :], ACT.Silu, scale=blk_inv[:, bass.ds(j, 1)])\
                        .then_inc(s_made, 1)

                def part_g(j, u):
                    after(act, y_made, j - 1)
                    act.wait_ge(gt_made, j + 1)
                    a.activation(gh[:, u, :], PS[:, 5, :], ACT.Copy).then_inc(gh_made, 1)

                def keep_y(j, u):
                    after(act, ye_out[u], 8 * (j - u))
                    act.wait_ge(y_made, j + 1)
                    a.activation(ye[:, u, :], PS[:, 6 + u, 0:D], ACT.Copy).then_inc(ye_made, 1)

                def first():
                    keep_zt(0, 0)
                    silu(0, 0)
                    keep_zt(1, 1)

                def step(j, u, more, more2):
                    if more:
                        silu(j + 1, 1 - u)
                    if not (isinstance(j, int) and j == NB):
                        part_g(j, u)
                    if more2:
                        keep_zt(j + 2, u)
                    if not (isinstance(j, int) and j == 0):
                        keep_y(j - 1, 1 - u)

                steps(act, first, step)

            @block.vector
            def _(dve):
                v = nc.vector

                def hidden(j, u):
                    after(dve, gt_made, j - 1)
                    dve.wait_ge(s_made, j + 1)
                    dve.wait_ge(h2_made, j + 1)
                    v.scalar_tensor_tensor(out=g[:, u, :], in0=PS[:, 2 + 2 * u, :], scalar=blk_inv[:, bass.ds(j, 1)],
                                           in1=s[:, u, :], op0=ALU.mult, op1=ALU.mult).then_inc(g_made, 1)

                def part_g(j, u):
                    after(dve, y_made, j - 1)
                    dve.wait_ge(gh_made, j + 1)
                    v.tensor_tensor(gl[:, u, :], PS[:, 5, :], gh[:, u, :].bitcast(F32), ALU.subtract)\
                        .then_inc(gl_made, 1)

                def first():
                    hidden(0, 0)

                def step(j, u, more, more2):
                    if more:
                        hidden(j + 1, 1 - u)
                    if not (isinstance(j, int) and j == NB):
                        part_g(j, u)

                steps(dve, first, step)


def attend1(nc, sem, PS, X1, ident, rowmask, prob, ye_idx, ye_dram, st3, cd, b3, b2b, b1, b2):
    st = ExitStack()
    with st:
        def sb(name, shape, dt=F32):
            return st.enter_context(nc.sbuf_tensor(name, shape, dt))

        b1b = sb("b1_rows", [P, F])
        bh, bl = sb("b1_high", [P, F], F32R), sb("b1_low", [P, F])
        row = sb("row_masks", [P, 1])
        cs = sb("c1_in", [P, R, D])
        idx = sb("row_places", [P, Q, 2], U32)
        rows = sb("expert_rows_in", [P, Q, 2, D])
        cqT = sb("c_and_q_T", [P, 2, 2 * D])
        qs = sb("q_neg", [P, R, D])
        ne = sb("neg_scores", [P, Q, P])
        least = sb("neg_max", [P, Q])
        pr = sb("exps", [P, Q, P])
        pT = sb("exps_T", [P, 2, P])
        total = sb("exp_sums", [P, Q])
        inv = sb("exp_invs", [P, Q])
        stt = sb("moments1_in", [P, R, 6])
        mean, var, rst, tmp, qsc, qbi = (sb(n, [P, R]) for n in (
            "means1", "vars1", "rstds1", "tmp1", "q_scales", "q_biases"))

        b_in = sem("b_in")
        b3_made = sem("b1_parts")
        c_in = [sem(f"c1_in{k}") for k in range(R)]
        r_in = [[sem(f"rows_in{k}{n}") for n in range(2)] for k in range(Q)]
        idx_made, x2_half, x2_made, x2_stat, norms_made, q_made = (sem("a1_" + n) for n in (
            "idx", "x2_half", "x2", "x2_stat", "norms", "q"))
        cq_made, cq_kept, sc_made, ne_made, p_made = (sem("a1_" + n) for n in (
            "cq_turned", "cq_kept", "scores", "neg_scores", "exps"))
        pt_made, pt_kept, inv_made, o_made, x3_made, x3_stat = (sem("a1_" + n) for n in (
            "pt_made", "pt_kept", "inverse", "out", "x3", "x3_stat"))
        LINKS = NORM_N + 2

        def at(i, k):
            return bass.ds(R * i + k, 1)

        def x_row(i, k):
            return X1[:, at(i, k), :].rearrange("p a d -> p (a d)")

        def schedule(eng, group):
            group(0)
            with eng.Fori(1, NR - 1) as i:
                group(i)
            group(NR - 1)
            group(NR)

        with nc.Block() as block:
            @block.sync
            def _(sp):
                def load(i, k):
                    after(sp, o_made, R * i + (k - (R - 1)))
                    sp.dma_start(cs[:, k, :], cd[:, at(i, k), :]).then_inc(c_in[k], 16)

                sp.dma_start(b1b[:, :], b1.partition_broadcast(P)).then_inc(b_in, 16)
                sp.dma_start(b2b[:, :], b2.partition_broadcast(P)).then_inc(b_in, 16)
                for k in range(R):
                    load(0, k)
                with sp.Fori(1, NR) as i:
                    for k in range(R):
                        load(i, k)
                sp.wait_ge(b_in, 32)

            @block.gpsimd
            def _(pool):
                def gathers(i):
                    for k in range(R):
                        m = k % Q
                        for n in range(2):
                            after(pool, r_in[m][n], 16 * (2 * i + k // Q))
                        apart(pool, x2_made, R * i + (k - 3))
                        pool.tensor_copy(idx[:, m, :], ye_idx[:, at(i, k), :].rearrange("p a n -> p (a n)"))\
                            .then_inc(idx_made, 1)
                        apart(pool, idx_made, R * i + (k + 1))
                        for n in range(2):
                            pool.indirect_dma_start(rows[:, m, n, :], None, ye_dram[:, :],
                                                    bass.IndirectOffsetOnAxis(ap=idx[:, m, n:n + 1], axis=0))\
                                .then_inc(r_in[m][n], 16)

                gathers(0)
                with pool.Fori(1, NR) as i:
                    gathers(i)

            @block.scalar
            def _(act):
                a = nc.scalar

                def make_q(i, k):
                    after(act, cq_made, R * i + (k - (R - 1)))
                    apart(act, norms_made, LINKS * (2 * i + (k // Q + 1)))
                    a.activation(qs[:, k, :], x_row(i, k), ACT.Identity, scale=qsc[:, k:k + 1],
                                 bias=qbi[:, k:k + 1]).then_inc(q_made, 1)

                def keep_turned(i, k):
                    after(act, sc_made, R * i + (k - 1))
                    act.wait_ge(cq_made, R * i + (k + 1))
                    a.activation(cqT[:, k % 2, :], PS[:, k % 2, :], ACT.Copy).then_inc(cq_kept, 1)

                def exps(i, k):
                    after(act, pt_made, R * i + (k - 3))
                    after(act, inv_made, R * i + (k - 3))
                    act.wait_ge(ne_made, R * i + (k + 1))
                    a.activation(pr[:, k % Q, :], ne[:, k % Q, :], ACT.Exp, scale=-1.0,
                                 bias=least[:, k % Q:k % Q + 1], accum_out=total[:, k % Q:k % Q + 1]).then_inc(p_made, 1)

                def keep_pt(i, k):
                    after(act, o_made, R * i + (k - 1))
                    act.wait_ge(pt_made, R * i + (k + 1))
                    a.activation(pT[:, k % 2, :], PS[:, 3, 0:P], ACT.Copy).then_inc(pt_kept, 1)

                def group(i):
                    for k in range(R):
                        at_tile(keep_turned, i, k, 0)
                        at_tile(make_q, i, k, -1)
                        at_tile(exps, i, k, 1)
                        at_tile(keep_pt, i, k, 2)

                make_q(0, 0)
                schedule(act, group)

            @block.tensor
            def _(pe):
                def turn(i, k):
                    after(pe, cq_kept, R * i + (k - 1))
                    pe.wait_ge(c_in[k], 16 * i + 16)
                    for c in range(DC):
                        pe.transpose(PS[:, k % 2, c * P:(c + 1) * P],
                                     cs[:, k, c * P:(c + 1) * P], ident[:, :])
                    pe.wait_ge(q_made, R * i + (k + 1))
                    for c in range(DC):
                        mm = pe.transpose(PS[:, k % 2, D + c * P:D + (c + 1) * P], qs[:, k, c * P:(c + 1) * P],
                                          ident[:, :])
                    mm.then_inc(cq_made, 1)

                def scores(i, k):
                    after(pe, ne_made, R * i + k)
                    pe.wait_ge(cq_kept, R * i + (k + 1))
                    for c in range(DC):
                        mm = pe.matmul(PS[:, 2, 0:P], cqT[:, k % 2, D + c * P:D + (c + 1) * P],
                                       cqT[:, k % 2, c * P:(c + 1) * P], start=(c == 0), stop=(c == DC - 1))
                    mm.then_inc(sc_made, 1)

                def turn_p(i, k):
                    after(pe, pt_kept, R * i + k)
                    pe.wait_ge(p_made, R * i + (k + 1))
                    pe.transpose(PS[:, 3, 0:P], pr[:, k % Q, :], ident[:, :]).then_inc(pt_made, 1)

                def product(i, k):
                    after(pe, x3_made, R * i + (k - 1))
                    pe.wait_ge(pt_kept, R * i + (k + 1))
                    pe.matmul(PS[:, 4 + k % 2, 0:D], pT[:, k % 2, :],
                              cs[:, k, :], start=True, stop=True)\
                        .then_inc(o_made, 1)

                def group(i):
                    for k in range(R):
                        at_tile(turn, i, k, 0)
                        at_tile(scores, i, k, 1)
                        at_tile(turn_p, i, k, 2)
                        at_tile(product, i, k, 3)

                schedule(pe, group)

            @block.vector
            def _(dve):
                v = nc.vector

                def sum_rows(i, k):
                    dve.wait_ge(r_in[k % Q][0], 16 * (2 * i + (k // Q + 1)))
                    v.scalar_tensor_tensor(out=x_row(i, k), in0=rows[:, k % Q, 0, :], scalar=prob[:, 0, at(i, k)],
                                           in1=x_row(i, k), op0=ALU.mult, op1=ALU.add).then_inc(x2_half, 1)

                def sum_rows2(i, k):
                    dve.wait_ge(r_in[k % Q][1], 16 * (2 * i + (k // Q + 1)))
                    dve.wait_ge(x2_half, R * i + (k + 1))
                    v.scalar_tensor_tensor(out=x_row(i, k), in0=rows[:, k % Q, 1, :], scalar=prob[:, 1, at(i, k)],
                                           in1=x_row(i, k), op0=ALU.mult, op1=ALU.add).then_inc(x2_made, 1)

                def moments_x(i, k):
                    apart(dve, x2_made, R * i + (k + 1))
                    v.bn_stats(stt[:, k, :], x_row(i, k)).then_inc(x2_stat, 1)

                def norms(i, half):
                    dve.wait_ge(x2_stat, R * i + (half + 1) * Q)
                    after(dve, q_made, R * i + (half * Q - Q))
                    ch = Chain(dve, norms_made, LINKS * (2 * i + half))
                    part = slice(half * Q, (half + 1) * Q)
                    yield from moments(v, ch, stt[:, part, :], mean[:, part], var[:, part], tmp[:, part])
                    ch.join()
                    ch.post(v.tensor_scalar(var[:, part], var[:, part], LN_EPS, None, ALU.add))
                    yield
                    yield from rsqrt_steps(v, ch, rst[:, part], var[:, part], tmp[:, part])
                    ch.join()
                    ch.post(v.tensor_scalar(qsc[:, part], rst[:, part], -1.0 / 16.0, None, ALU.mult))
                    yield
                    ch.join()
                    ch.post(v.scalar_tensor_tensor(out=qbi[:, part], in0=mean[:, part], scalar=-1.0, in1=qsc[:, part],
                                                   op0=ALU.mult, op1=ALU.mult))
                    assert ch.n == LINKS

                def masked(i, k):
                    after(dve, p_made, R * i + (k - 3))
                    dve.wait_ge(sc_made, R * i + (k + 1))
                    v.tensor_scalar(ne[:, k % Q, :], PS[:, 2, 0:P], rowmask[:, at(i, k)], HUGE, ALU.add, ALU.min,
                                    accum_out=least[:, k % Q:k % Q + 1]).then_inc(ne_made, 1)

                def invert(i, k):
                    after(dve, x3_made, R * i + (k - 3))
                    dve.wait_ge(p_made, R * i + (k + 1))
                    v.reciprocal(inv[:, k % Q:k % Q + 1], total[:, k % Q:k % Q + 1]).then_inc(inv_made, 1)

                def add_out(i, k):
                    dve.wait_ge(o_made, R * i + (k + 1))
                    dve.wait_ge(inv_made, R * i + (k + 1))
                    v.scalar_tensor_tensor(out=x_row(i, k), in0=PS[:, 4 + k % 2, 0:D], scalar=inv[:, k % Q:k % Q + 1],
                                           in1=x_row(i, k), op0=ALU.mult, op1=ALU.add).then_inc(x3_made, 1)

                def moments_x3(i, k):
                    apart(dve, x3_made, R * i + (k + 1))
                    v.bn_stats(st3[:, at(i, k), :].rearrange("p a s -> p (a s)"), x_row(i, k)).then_inc(x3_stat, 1)

                def front(i, half):
                    for k in range(half * Q, (half + 1) * Q):
                        sum_rows(i, k)
                        if k % Q >= 1:
                            sum_rows2(i, k - 1)
                    sum_rows2(i, half * Q + Q - 1)
                    for k in range(half * Q, (half + 1) * Q):
                        moments_x(i, k)

                def group(i):
                    for k in range(R):
                        half, m = divmod(k, Q)
                        if m == 0:
                            chain = iter(())
                            if not isinstance(i, int) or i < NR - 1 or (i == NR - 1 and half == 0):
                                chain = norms(i, 1) if half == 0 else norms(i + 1, 0)
                        at_tile(masked, i, k, 1)
                        advance(chain, 1)
                        if m >= 1:
                            at_tile(sum_rows2, i, k, 1 - R)
                            advance(chain, 1)
                        at_tile(add_out, i, k, 4)
                        advance(chain, 1)
                        at_tile(invert, i, k, 3)
                        advance(chain, 1)
                        at_tile(moments_x3, i, k, 5)
                        advance(chain, 1 if m < 3 else LINKS)
                        at_tile(sum_rows, i, k, -R)
                        if m == 3:
                            at_tile(sum_rows2, i, k, -R)
                            for n in range(k - 3, k + 1):
                                at_tile(moments_x, i, n, -R)

                v.tensor_tensor(row[:, :], ident[:, 0:1], ident[:, 2:3], ALU.add).then_inc(b3_made, 1)
                dve.wait_ge(b_in, 32)
                v.tensor_copy(bh[:, :], b1b[:, :]).then_inc(b3_made, 1)
                dve.wait_ge(b3_made, 2)
                v.tensor_tensor(bl[:, :], b1b[:, :], bh[:, :].bitcast(F32), ALU.subtract).then_inc(b3_made, 1)
                dve.wait_ge(b3_made, 3)
                v.tensor_scalar(bl[:, :], bl[:, :], ident[:, 1:2], None, ALU.mult).then_inc(b3_made, 1)
                dve.wait_ge(b3_made, 4)
                v.scalar_tensor_tensor(out=b3[:, :], in0=bh[:, :].bitcast(F32), scalar=row[:, 0:1], in1=bl[:, :],
                                       op0=ALU.mult, op1=ALU.add).then_inc(b3_made, 1)
                front(0, 0)
                advance(norms(0, 0), LINKS)
                front(0, 1)
                schedule(dve, group)
                dve.wait_ge(x3_stat, T)


def bitffn(nc, sem, PS, X1, ident, magic, wmean, w1q, w2q, b3, b2b, st3, od):
    st = ExitStack()
    with st:
        def sb(name, shape, dt=F32):
            return st.enter_context(nc.sbuf_tensor(name, shape, dt))

        d = sb("x_centred", [P, R, D])
        xb = sb("x_plus_b2", [P, R, D])
        t1 = sb("x_rounded", [P, Q, D])
        x1T = sb("x_whole_T", [P, 2, DC * P], BF16)
        h = sb("hidden_ffn", [P, R, F])
        junk = sb("squares", [P, F], BF16)
        t2 = sb("h_rounded", [P, 2, F])
        hT = sb("h_whole_T", [P, 2, FC * P], BF16)
        fin = sb("rows_out", [P, Q, D])
        mean, var, rst, tmp = (sb("ffn_" + n, [P, T]) for n in ("mean", "var", "rst", "tmp"))
        am, a1, ss, r2, v2, tm2, a2 = (sb("ffn_" + n, [P, Q]) for n in (
            "amax", "clip", "squares", "rst2", "var2", "tmp2", "clip2"))
        k1, al, be, am2, k2 = (sb("ffn_" + n, [P, R]) for n in ("k1", "alpha", "beta", "amax2", "k2"))
        ial = sb("ffn_alpha_inv", [P, Q])
        ial3 = sb("ffn_alpha_inv_parts", [P, Q, 3], F32R)
        ialT = sb("ffn_alpha_inv_T", [P, 2, Q * P], F32R)

        norms_made, d_made, xb_made, am_made, t1_made, links1 = (sem("f_" + n) for n in (
            "norms", "centred", "x_b2", "amax", "x_rounded", "links1"))
        xt_made, xt_kept, h_made, gelu_made, sq_made, am2_made = (sem("f_" + n) for n in (
            "xt_made", "xt_kept", "h_psum", "gelu", "squares", "amax2"))
        links2, t2_made, ht_made, ht_kept, y_made, fin_made = (sem("f_" + n) for n in (
            "links2", "h_rounded", "ht_made", "ht_kept", "y_psum", "final"))
        o_out = [sem(f"out_stored{k}") for k in range(Q)]
        bt_zero, bt_made, bt_kept = (sem("f_" + n) for n in ("alpha_zeroed", "alpha_turned", "alpha_kept"))
        L1 = 9
        L2 = 1 + RSQRT_N + 5

        def at(i, k):
            return bass.ds(R * i + k, 1)

        def x_row(i, k):
            return X1[:, at(i, k), :].rearrange("p a d -> p (a d)")

        def schedule(eng, group):
            group(0)
            with eng.Fori(1, NR - 1) as i:
                group(i)
            group(NR - 1)
            group(NR)

        with nc.Block() as block:
            @block.sync
            def _(sp):
                def store(i, k):
                    sp.wait_ge(fin_made, R * i + (k + 1))
                    sp.dma_start(od[:, at(i, k), :], fin[:, k % Q, :]).then_inc(o_out[k % Q], 16)

                with sp.Fori(0, NR) as i:
                    for k in range(R):
                        store(i, k)
                for k in range(Q):
                    sp.wait_ge(o_out[k], 16 * NQ)

            @block.gpsimd
            def _(pool):
                def centre(i, k):
                    apart(pool, t1_made, R * i + (k - (R - 1)))
                    pool.tensor_tensor(d[:, k, :], x_row(i, k), mean[:, at(i, k)].broadcast_to([P, D]), ALU.subtract)\
                        .then_inc(d_made, 1)

                def add_b2(i, k):
                    apart(pool, fin_made, R * i + (k - (Q - 1)))
                    pool.tensor_tensor(xb[:, k, :], x_row(i, k), b2b[:, :], ALU.add).then_inc(xb_made, 1)

                def round_x(i, k):
                    apart(pool, xt_made, R * i + (k - 3))
                    apart(pool, links1, L1 * (2 * i + (k // Q + 1)))
                    pool.tensor_scalar(t1[:, k % Q, :], d[:, k, :], k1[:, k:k + 1], ROUND, ALU.mult, ALU.add)\
                        .then_inc(t1_made, 1)

                def group(i):
                    for k in range(R):
                        at_tile(round_x, i, k, -3)
                        at_tile(centre, i, k, -R)
                        at_tile(add_b2, i, k, Q)

                pool.wait_ge(norms_made, NORM_N)
                for k in range(R):
                    centre(0, k)
                for k in range(3):
                    round_x(0, k)
                schedule(pool, group)

            @block.scalar
            def _(act):
                a = nc.scalar

                def keep_xt(i, k):
                    after(act, h_made, R * i + (k - 1))
                    act.wait_ge(xt_made, R * i + (k + 1))
                    a.activation(x1T[:, k % 2, :], PS[:, 0, 0:D], ACT.Identity, bias=magic[:, 1:2]).then_inc(xt_kept, 1)

                def gelu(i, k):
                    after(act, t2_made, R * i + (k - (R - 1)))
                    act.wait_ge(h_made, R * i + (k + 1))
                    a.activation(h[:, k, :], PS[:, 1:3, :].rearrange("p a b -> p (a b)"), ACT.Gelu,
                                 scale=al[:, k:k + 1]).then_inc(gelu_made, 1)

                def square(i, k):
                    after(act, sq_made, R * i + k)
                    if k % Q == 0:
                        after(act, links2, L2 * (2 * i + (k // Q - 1)) + 1)
                    apart(act, gelu_made, R * i + (k + 1))
                    a.activation(junk[:, :], h[:, k, :], ACT.Square, accum_out=ss[:, k % Q:k % Q + 1]).then_inc(sq_made, 1)

                def keep_ht(i, k):
                    after(act, y_made, R * i + (k - 1))
                    act.wait_ge(ht_made, R * i + (k + 1))
                    a.activation(hT[:, k % 2, :], PS[:, 3:5, :].rearrange("p a b -> p (a b)"), ACT.Identity,
                                 bias=magic[:, 1:2]).then_inc(ht_kept, 1)

                def group(i):
                    for k in range(R):
                        at_tile(keep_xt, i, k, -1)
                        at_tile(square, i, k, 1)
                        at_tile(gelu, i, k, 0)
                        at_tile(keep_ht, i, k, 7)

                keep_xt(0, 0)
                schedule(act, group)

            @block.tensor
            def _(pe):
                def turn_x(i, k):
                    after(pe, xt_kept, R * i + k)
                    pe.wait_ge(t1_made, R * i + (k + 1))
                    for c in range(DC):
                        mm = pe.transpose(PS[:, 0, c * P:(c + 1) * P], t1[:, k % Q, c * P:(c + 1) * P], ident[:, :])
                    mm.then_inc(xt_made, 1)

                def turn_b(i, k):
                    half = k // Q
                    pe.wait_ge(links1, L1 * (2 * i + (half + 1)))
                    after(pe, bt_kept, 2 * i + half)
                    for n in range(Q):
                        mm = pe.transpose(PS[0:3, 7, n * P:(n + 1) * P], ial3[:, n, :].bitcast(F32), ident[:, :])
                    mm.then_inc(bt_made, 1)

                def up(i, k):
                    if k % Q == 0:
                        pe.wait_ge(bt_kept, 2 * i + (k // Q + 1))
                    after(pe, gelu_made, R * i + k)
                    pe.wait_ge(xt_kept, R * i + (k + 1))
                    for c in range(DC):
                        for half in range(2):
                            pe.matmul(PS[:, 1 + half, :], x1T[:, k % 2, c * P:(c + 1) * P],
                                      w1q[:, c, half * 512:(half + 1) * 512], start=(c == 0), stop=False)
                    for half in range(2):
                        mm = pe.matmul(PS[:, 1 + half, :], ialT[:, k // Q, (k % Q) * P:(k % Q + 1) * P],
                                       b3[:, half * 512:(half + 1) * 512], start=False, stop=True)
                    mm.then_inc(h_made, 1)

                def turn_h(i, k):
                    after(pe, ht_kept, R * i + k)
                    pe.wait_ge(t2_made, R * i + (k + 1))
                    for c in range(FC):
                        mm = pe.transpose(PS[:, 3 + c // 4, (c % 4) * P:(c % 4 + 1) * P],
                                          t2[:, k % 2, c * P:(c + 1) * P], ident[:, :])
                    mm.then_inc(ht_made, 1)

                def down(i, k):
                    after(pe, fin_made, R * i + max(k - 1, 0))
                    pe.wait_ge(ht_kept, R * i + (k + 1))
                    for c in range(FC):
                        mm = pe.matmul(PS[:, 5 + k % 2, 0:D], hT[:, k % 2, c * P:(c + 1) * P], w2q[:, c, :],
                                       start=(c == 0), stop=(c == FC - 1))
                    mm.then_inc(y_made, 1)

                def group(i):
                    for k in range(R):
                        at_tile(turn_x, i, k, -1)
                        at_tile(up, i, k, 0)
                        at_tile(down, i, k, 8)
                        at_tile(turn_h, i, k, 7)
                        if k % Q == 1:
                            at_tile(turn_b, i, k, -3)

                turn_x(0, 0)
                turn_b(0, 0)
                schedule(pe, group)

            @block.vector
            def _(dve):
                v = nc.vector

                def norms():
                    ch = Chain(dve, norms_made, 0)
                    yield from moments(v, ch, st3[:, :, :], mean[:, :], var[:, :], tmp[:, :])
                    ch.join()
                    ch.post(v.tensor_scalar(var[:, :], var[:, :], 1.0 + RMS_EPS, RMS_EPS * LN_EPS, ALU.mult, ALU.add))
                    yield
                    yield from rsqrt_steps(v, ch, rst[:, :], var[:, :], tmp[:, :])
                    ch.join()
                    assert ch.n == NORM_N

                def largest_x(i, k):
                    dve.wait_ge(d_made, R * i + (k + 1))
                    v.tensor_reduce(am[:, k % Q:k % Q + 1], d[:, k, :], AX_X, ALU.max, apply_absolute_value=True)\
                        .then_inc(am_made, 1)

                def scale_x(i, half):
                    first = R * i + half * Q
                    dve.wait_ge(am_made, R * i + (half + 1) * Q)
                    after(dve, t1_made, first - Q)
                    after(dve, gelu_made, first - Q)
                    after(dve, bt_made, 2 * i + half)
                    ch = Chain(dve, links1, L1 * (2 * i + half))
                    rst_i = rst[:, bass.ds(first, Q)]
                    ch.post(v.tensor_tensor(a1[:, :], am[:, :], rst_i, ALU.mult))
                    yield
                    ch.join()
                    ch.post(v.tensor_scalar(a1[:, :], a1[:, :], QUANT_EPS, 1.0 / 127.0, ALU.max, ALU.mult))
                    yield
                    ch.join()
                    ch.post(v.tensor_scalar(al[:, half * Q:half * Q + Q], a1[:, :], wmean[:, 0:1], None, ALU.mult))
                    ch.post(v.reciprocal(k1[:, half * Q:half * Q + Q], a1[:, :]))
                    yield
                    ch.join()
                    ch.post(v.tensor_tensor(k1[:, half * Q:half * Q + Q], k1[:, half * Q:half * Q + Q], rst_i, ALU.mult))
                    ch.post(v.reciprocal(ial[:, :], al[:, half * Q:half * Q + Q]))
                    yield
                    ch.join()
                    ch.post(v.tensor_copy(ial3[:, :, 0], ial[:, :]))
                    ch.post(v.tensor_copy(ial3[:, :, 1], ial[:, :]))
                    yield
                    ch.join()
                    ch.post(v.tensor_tensor(ial3[:, :, 2], ial[:, :], ial3[:, :, 0].bitcast(F32), ALU.subtract))
                    assert ch.n == L1

                def keep_b(i, k):
                    half = k // Q
                    after(dve, h_made, R * i + (half * Q - Q))
                    dve.wait_ge(bt_made, 2 * i + (half + 1))
                    v.tensor_copy(ialT[0:3, half, :], PS[0:3, 7, :]).then_inc(bt_kept, 1)

                def largest_h(i, k):
                    apart(dve, gelu_made, R * i + (k + 1))
                    v.tensor_reduce(am2[:, k:k + 1], h[:, k, :], AX_X, ALU.max, apply_absolute_value=True)\
                        .then_inc(am2_made, 1)

                def scale_h(i, half):
                    dve.wait_ge(am2_made, R * i + (half + 1) * Q)
                    dve.wait_ge(sq_made, R * i + (half + 1) * Q)
                    after(dve, t2_made, R * i + (half - 1) * Q)
                    after(dve, fin_made, R * i + (half - 1) * Q)
                    ch = Chain(dve, links2, L2 * (2 * i + half))
                    ch.post(v.tensor_scalar(v2[:, :], ss[:, :], 1.0 / F, RMS_EPS, ALU.mult, ALU.add))
                    yield
                    yield from rsqrt_steps(v, ch, r2[:, :], v2[:, :], tm2[:, :])
                    ch.join()
                    ch.post(v.tensor_tensor(a2[:, :], am2[:, half * Q:half * Q + Q], r2[:, :], ALU.mult))
                    yield
                    ch.join()
                    ch.post(v.tensor_scalar(a2[:, :], a2[:, :], QUANT_EPS, 1.0 / 127.0, ALU.max, ALU.mult))
                    yield
                    ch.join()
                    ch.post(v.tensor_scalar(be[:, half * Q:half * Q + Q], a2[:, :], wmean[:, 1:2], None, ALU.mult))
                    ch.post(v.reciprocal(k2[:, half * Q:half * Q + Q], a2[:, :]))
                    yield
                    ch.join()
                    ch.post(v.tensor_tensor(k2[:, half * Q:half * Q + Q], k2[:, half * Q:half * Q + Q], r2[:, :], ALU.mult))
                    assert ch.n == L2

                def round_h(i, k):
                    after(dve, ht_made, R * i + (k - 1))
                    dve.wait_ge(links2, L2 * (2 * i + (k // Q + 1)))
                    v.tensor_scalar(t2[:, k % 2, :], h[:, k, :], k2[:, k:k + 1], ROUND, ALU.mult, ALU.add)\
                        .then_inc(t2_made, 1)

                def finish(i, k):
                    after(dve, o_out[k % Q], 16 * (2 * i + k // Q))
                    dve.wait_ge(xb_made, R * i + (k + 1))
                    dve.wait_ge(y_made, R * i + (k + 1))
                    v.scalar_tensor_tensor(out=fin[:, k % Q, :], in0=PS[:, 5 + k % 2, 0:D], scalar=be[:, k:k + 1],
                                           in1=xb[:, k, :], op0=ALU.mult, op1=ALU.add).then_inc(fin_made, 1)

                def group(i):
                    for k in range(R):
                        half, m = divmod(k, Q)
                        if m == 0:
                            chain_h, chain_x = [], []
                            at_tile(lambda ii, kk: chain_h.append(scale_h(ii, kk // Q)), i, k, Q)
                            at_tile(lambda ii, kk: chain_x.append(scale_x(ii, kk // Q)), i, k, -Q)
                            chain_h = chain_h[0] if chain_h else iter(())
                            chain_x = chain_x[0] if chain_x else iter(())
                        at_tile(round_h, i, k, 7)
                        if m == 2:
                            at_tile(keep_b, i, k, -2)
                        if m > 0:
                            advance(chain_h, 2)
                        at_tile(largest_h, i, k, 1)
                        if m == 0:
                            for _ in range(6):
                                advance(chain_x, 1)
                                advance(chain_h, 1)
                        else:
                            advance(chain_h, 2)
                        at_tile(finish, i, k, 8)
                        if m > 0:
                            advance(chain_h, 2)
                        if m == 2:
                            at_tile(largest_x, i, k, -6)
                            advance(chain_h, 2)
                            at_tile(largest_x, i, k, -7)
                            advance(chain_h, L2)
                        if m == 3:
                            at_tile(largest_x, i, k, -7)
                            at_tile(largest_x, i, k, -8)

                advance(norms(), NORM_N)
                v.memset(ialT[:, :, :].bitcast(F32), 0.0).then_inc(bt_zero, 1)
                for k in range(Q):
                    largest_x(0, k)
                advance(scale_x(0, 0), L1)
                for k in range(Q, R):
                    largest_x(0, k)
                dve.wait_ge(bt_zero, 1)
                keep_b(0, 0)
                schedule(dve, group)


_INS = ['x', 'ctx_1024', 'mask_BxS_bk1', 'L0_ffn_w12', 'L0_ffn_w3', 'L0_ffn_gate_w', 'L1_ffn_w1', 'L1_ffn_b1',
        'L1_ffn_w2', 'L1_ffn_b2']


def kernel(**inputs):
    import numpy as np
    import concourse.bacc as bacc
    from concourse.bass_utils import run_bass_kernel_spmd

    nc = bacc.Bacc("TRN2", target_bir_lowering=False, num_devices=1)
    arrays, args = {}, []
    for name in _INS:
        a = np.ascontiguousarray(inputs[name])
        arrays[f"in_{name}"] = a
        args.append(nc.dram_tensor(f"in_{name}", a.shape, mybir.dt.from_np(a.dtype), kind="ExternalInput").ap())
    out = nc.dram_tensor("out", (T, P, D), F32, kind="ExternalOutput").ap()
    build(nc, *args, out)
    r = run_bass_kernel_spmd(nc, [arrays], core_ids=[0])
    return r.results[0]["out"]
```
